# Optimizing a Trainium2 kernel written in Bass

```python
import numpy as np
import jax
import jax.numpy as jnp

def _softmax(x, axis=-1):
    return jax.nn.softmax(x, axis=axis)

def _gelu(x):
    return jax.nn.gelu(x, approximate=True)

def _silu(x):
    return jax.nn.silu(x)

def _sigmoid(x):
    return jax.nn.sigmoid(x)

def _layernorm(x, axis=-1, eps=1e-05):
    m = jnp.mean(x, axis=axis, keepdims=True)
    v = jnp.var(x, axis=axis, keepdims=True)
    return (x - m) / jnp.sqrt(v + eps)

def _scatter_add(tgt, idx, src, axis=0):
    return tgt.at[idx].add(src)

def _segment_sum(src, seg, n):
    return jax.ops.segment_sum(src, seg, n)
kernel_name = 'mk_adj_resnorm_d2_adj_r2_5a2d00'

def setup_inputs(seed: int=0):
    np.random.seed(seed)
    _w = jnp.asarray

    def _rec_inputs():
        import jax
        import jax.numpy as jnp
        _gk = jax.random.key(seed)
        x = -0.0003929 + 0.9999 * jax.random.normal(jax.random.fold_in(_gk, 1), (32, 256, 512), jnp.float32)
        _a = jax.random.bernoulli(jax.random.fold_in(_gk, 2), 0.0625, (256, 256))
        _a = jnp.logical_or(_a, jnp.swapaxes(_a, -1, -2))
        _a = jnp.logical_or(_a, jnp.eye(256, dtype=bool))
        _af = _a.astype(jnp.float32)
        _af = _af * jax.random.uniform(jax.random.fold_in(_gk, 3), (256, 256), jnp.float32, 0.05, 0.198159)
        adj = _af
        return (x, adj)
    x, adj = _rec_inputs()

    def _L0_gnn_setup():
        import jax, jax.numpy as jnp
        import numpy as np
        NEG_SLOPE = 0.01
        key = jax.random.key(seed)
        k1, k2, k3, k4, k5 = jax.random.split(key, 5)
        B, C, N, O = (32, 256, 512, 256)
        x = jax.random.normal(k1, (B, C, N), dtype=jnp.float32)
        wq = jax.random.normal(k2, (C,), dtype=jnp.float32) * (1.0 / np.sqrt(C))
        wk = jax.random.normal(k3, (C,), dtype=jnp.float32) * (1.0 / np.sqrt(C))
        wm = jax.random.normal(k4, (O, C), dtype=jnp.float32) * (1.0 / np.sqrt(C))
        bm = jax.random.normal(k5, (O,), dtype=jnp.float32) * 0.01
        return {'x': x, 'wq': wq, 'wk': wk, 'wm': wm, 'bm': bm}
    _L0_gnn_all = _L0_gnn_setup()
    _L0_gnn_in = {k: v for k, v in _L0_gnn_all.items() if k in ('wq', 'wk', 'bm')}
    del _L0_gnn_all

    def _L1_gnn_setup():
        import jax, jax.numpy as jnp
        import numpy as np
        EPS = 1e-08

        def _row_stochastic_causal(A, causal_mask):
            A = A * causal_mask
            deg = jnp.maximum(A.sum(axis=-1, keepdims=True), EPS)
            return A / deg
        key = jax.random.key(seed)
        k = jax.random.split(key, 5)
        B, N, D = (4, 1024, 512)
        s = 1.0 / np.sqrt(D)
        h = jax.random.normal(k[0], (B, N, D), dtype=jnp.float32)
        W_lang = jax.random.normal(k[1], (D, D), dtype=jnp.float32) * s
        W_grav = jax.random.normal(k[2], (D, D), dtype=jnp.float32) * s
        W_V = jax.random.normal(k[3], (D, D), dtype=jnp.float32) * s
        W_O = jax.random.normal(k[4], (D, D), dtype=jnp.float32) * s
        causal_mask = jnp.tril(jnp.ones((N, N), dtype=jnp.float32))
        gate_logit = jnp.zeros((), jnp.float32)
        log_sigma = jnp.zeros((), jnp.float32)
        return {'h': h, 'causal_mask': causal_mask, 'W_lang': W_lang, 'W_grav': W_grav, 'W_V': W_V, 'W_O': W_O, 'gate_logit': gate_logit, 'log_sigma': log_sigma}
    _L1_gnn_all = _L1_gnn_setup()
    _L1_gnn_in = {k: v for k, v in _L1_gnn_all.items() if k in ('W_lang', 'W_grav', 'W_V', 'W_O', 'gate_logit', 'log_sigma')}
    del _L1_gnn_all
    return {'x': x, 'adj': adj, 'L0_gnn_wq': _L0_gnn_in['wq'], 'L0_gnn_wk': _L0_gnn_in['wk'], 'L0_gnn_bm': _L0_gnn_in['bm'], 'L1_gnn_W_lang': _L1_gnn_in['W_lang'], 'L1_gnn_W_grav': _L1_gnn_in['W_grav'], 'L1_gnn_W_V': _L1_gnn_in['W_V'], 'L1_gnn_W_O': _L1_gnn_in['W_O'], 'L1_gnn_gate_logit': _L1_gnn_in['gate_logit'], 'L1_gnn_log_sigma': _L1_gnn_in['log_sigma']}

def reference(x, adj, L0_gnn_wq, L0_gnn_wk, L0_gnn_bm, L1_gnn_W_lang, L1_gnn_W_grav, L1_gnn_W_V, L1_gnn_W_O, L1_gnn_gate_logit, L1_gnn_log_sigma):
    import jax
    import jax.numpy as jnp

    def _L0_gnn_ref(x, wq, wk, wm, bm):
        import jax, jax.numpy as jnp
        import numpy as np
        NEG_SLOPE = 0.01
        q = jnp.einsum('c,bcn->bn', wq, x)
        k = jnp.einsum('c,bcn->bn', wk, x)
        scores = q[:, None, :] + k[:, :, None]
        scores = jnp.where(scores > 0, scores, NEG_SLOPE * scores)
        att = jax.nn.softmax(scores, axis=-1)
        agg = jnp.einsum('bcn,bmn->bcm', x, att)
        out = jnp.einsum('oc,bcm->bom', wm, agg) + bm[None, :, None]
        return jax.nn.relu(out)

    def _L1_gnn_ref(h, causal_mask, W_lang, W_grav, W_V, W_O, gate_logit, log_sigma):
        import jax, jax.numpy as jnp
        import numpy as np
        EPS = 1e-08

        def _row_stochastic_causal(A, causal_mask):
            A = A * causal_mask
            deg = jnp.maximum(A.sum(axis=-1, keepdims=True), EPS)
            return A / deg
        z_l = jnp.einsum('bnd,ed->bne', h, W_lang)
        z_g = jnp.einsum('bnd,ed->bne', h, W_grav)
        v = jnp.einsum('bnd,ed->bne', h, W_V)
        N = h.shape[-2]
        not_eye = 1.0 - jnp.eye(N, dtype=h.dtype)
        zn = z_l / jnp.maximum(jnp.linalg.norm(z_l, axis=-1, keepdims=True), EPS)
        A_l = jnp.maximum(jnp.einsum('bnd,bmd->bnm', zn, zn), 0.0) * not_eye
        sq = jnp.sum(z_g * z_g, axis=-1, keepdims=True)
        d2 = jnp.maximum(sq + jnp.swapaxes(sq, -1, -2) - 2.0 * jnp.einsum('bnd,bmd->bnm', z_g, z_g), 0.0)
        sigma = jnp.exp(log_sigma)
        A_g = jnp.exp(-d2 / (2.0 * sigma * sigma)) * not_eye
        K_l = _row_stochastic_causal(A_l, causal_mask)
        K_g = _row_stochastic_causal(A_g, causal_mask)
        w_l = jax.nn.sigmoid(gate_logit)
        K = w_l * K_l + (1.0 - w_l) * K_g
        out = jnp.einsum('bnm,bmd->bnd', K, v)
        return jnp.einsum('bnd,ed->bne', out, W_O)
    x = _layernorm(x + _L0_gnn_ref(x, L0_gnn_wq, L0_gnn_wk, adj, L0_gnn_bm), axis=-1)
    x = _layernorm(x + _L1_gnn_ref(x, adj, L1_gnn_W_lang, L1_gnn_W_grav, L1_gnn_W_V, L1_gnn_W_O, L1_gnn_gate_logit, L1_gnn_log_sigma), axis=-1)
    return x

_drawn_inputs = setup_inputs


def setup_inputs(seed=0):
    import zlib

    import numpy as np

    out = dict(_drawn_inputs(seed))
    spreads = {}
    factors = {'L0_gnn_wq': 6.186, 'L0_gnn_wk': 5.607, 'L0_gnn_bm': 200.0}
    for name, (base, spread) in spreads.items():
        noise = np.random.default_rng([zlib.crc32(name.encode()), seed]).standard_normal(out[name].shape)
        drawn = base * np.exp(spread * noise) if base else spread * noise
        out[name] = jnp.asarray(drawn.astype(out[name].dtype))
    for name, factor in factors.items():
        out[name] = (out[name] * factor).astype(out[name].dtype)
    return out
```

```python
from contextlib import ExitStack

import concourse.bass as bass
from concourse import mybir

F32 = mybir.dt.float32
F16 = mybir.dt.float16
ALU = mybir.AluOpType
ACT = mybir.ActivationFunctionType
AX = mybir.AxisListType
RMAX = bass.bass_isa.ReduceOp.max

P = 128
LN_EPS = 1e-5
DEG_EPS = 1e-8
NORM_EPS2 = 1e-16
SLOPE = 0.01
TOP = 4.0
LN256 = 5.545177444479562


def wait(engine, semaphore, count):
    if not (isinstance(count, int) and count <= 0):
        engine.wait_ge(semaphore, count)


def build(nc, x, adj, adjT, wq, wk, bm, wlT, wgT, wv, woT, gate, sigma, out):
    B, C, N = x.shape
    O = adj.shape[0]
    D = wlT.shape[0]
    PAIRS = B // 2
    CC, OC, NC, DC = C // P, O // P, N // P, D // P
    assert C == O == 2 * P and N == D == 4 * P

    x_v = x.rearrange("(t j) (c p) n -> t p j c n", j=2, p=P)
    out_v = out.rearrange("(t j) (c p) n -> t j p c n", j=2, p=P)

    with ExitStack() as ctx:
        def sb(name, shape, dt=F32):
            return ctx.enter_context(nc.sbuf_tensor(name, [P, *shape], dt))

        def sem(name):
            return ctx.enter_context(nc.semaphore(name))

        ident = sb("ident", [P])
        ones = sb("ones", [P])
        neg_ones = sb("neg_ones", [P])
        mask = sb("mask", [OC, O])
        exponent = sb("exponent", [4])
        shift = sb("shift", [1])
        bias_m = sb("bias_m", [OC])
        wl_hi, wl_lo = sb("wl_hi", [DC, D], F16), sb("wl_lo", [DC, D], F16)
        wg_hi, wg_lo = sb("wg_hi", [DC, D], F16), sb("wg_lo", [DC, D], F16)
        wvo_hi, wvo_lo = sb("wvo_hi", [DC, D], F16), sb("wvo_lo", [DC, D], F16)
        wm_hi, wm_lo = sb("wm_hi", [CC, O], F16), sb("wm_lo", [CC, O], F16)
        wq_hi, wq_lo = sb("wq_hi", [CC, 1], F16), sb("wq_lo", [CC, 1], F16)
        wk_hi, wk_lo = sb("wk_hi", [CC, P], F16), sb("wk_lo", [CC, P], F16)
        qk_raw = sb("qk_raw", [2, CC])
        knobs = sb("knobs", [2])
        wk_rep = sb("wk_rep", [CC, P])
        top_part, top_all = sb("top_part", [8]), sb("top_all", [8])
        scale = sb("scale", [8])
        unscale = sb("unscale", [8])
        c_u, c_v, c_a, c_b = (sb(n, [1]) for n in ("c_u", "c_v", "c_a", "c_b"))
        c_grav, c_wl, c_wg, c_out = (sb(n, [1]) for n in ("c_grav", "c_wl", "c_wg", "c_out"))
        c_norm = sb("c_norm", [4])
        tiny = sb("tiny", [8])
        eps = sb("eps", [4])
        turn_q, turn_y, turn_o = sb("turn_q", [2]), sb("turn_y", [1]), sb("turn_o", [1])
        x_in = sb("x_in", [2, CC, N])
        x_res = sb("x_res", [2, CC, N])
        x_hi, x_lo = sb("x_hi", [2, CC, N], F16), sb("x_lo", [2, CC, N], F16)
        OW = O + 2
        xw_hi, xw_lo = sb("xw_hi", [2, NC, OW], F16), sb("xw_lo", [2, NC, OW], F16)
        q_part, q_max, q_rel = sb("q_part", [2]), sb("q_max", [2]), sb("q_rel", [2, NC])
        u_col, v_col = sb("u_col", [2, NC]), sb("v_col", [2, NC])
        a_row, b_row = sb("a_row", [2, N]), sb("b_row", [2, N])
        vb = sb("vb", [2, N])
        att = sb("att", [2, N])
        att_hi, att_lo = sb("att_hi", [2, NC, N], F16), sb("att_lo", [2, NC, N], F16)
        den_inv = sb("den_inv", [8])
        agg_t = sb("agg_t", [2, NC, O])
        y = sb("y", [2 * OC, N])
        y_stat, y_mv = sb("y_stat", [2 * OC, 6]), sb("y_mv", [2 * OC, 2])
        y_var, y_rstd = sb("y_var", [2 * OC]), sb("y_rstd", [2 * OC])
        h = sb("h", [2 * OC, N])
        ht_hi, ht_lo = sb("ht_hi", [DC, 2 * O], F16), sb("ht_lo", [DC, 2 * O], F16)
        z_hi, z_lo = sb("z_hi", [2 * DC, 2 * O], F16), sb("z_lo", [2 * DC, 2 * O], F16)
        v_hi, v_lo = sb("v_hi", [2 * OC, D], F16), sb("v_lo", [2 * OC, D], F16)
        diag_junk = sb("diag_junk", [4, P])
        sq_l, sq_lc, r_l = sb("sq_l", [4]), sb("sq_lc", [4]), sb("r_l", [4])
        diag_g, sq_g = sb("diag_g", [2, O]), sb("sq_g", [4])
        diag_r = sb("diag_r", [4, P])
        a_l, a_g = sb("a_l", [2, OC, O]), sb("a_g", [2, OC, O])
        deg_l, deg_l2, deg_l3, deg_l4, s_l = (sb(n, [4]) for n in ("deg_l", "deg_l2", "deg_l3", "deg_l4", "s_l"))
        deg_g, deg_g2, deg_g3, s_g = (sb(n, [4]) for n in ("deg_g", "deg_g2", "deg_g3", "s_g"))
        kt_hi, kt_lo = sb("kt_hi", [2, OC, O], F16), sb("kt_lo", [2, OC, O], F16)
        o = sb("o", [2 * OC, N])
        o_stat, o_mv = sb("o_stat", [2 * OC, 6]), sb("o_mv", [2 * OC, 2])
        o_var, o_rstd = sb("o_var", [2 * OC]), sb("o_rstd", [2 * OC])
        wl_raw = agg_t[:].rearrange("p j c n -> p (j c n)").rearrange("p (c n) -> p c n", c=DC)
        wg_raw, wv_raw, wo_raw = y[:], o[:], h[:]
        adjT_raw = att[:].rearrange("p a n -> p (a n)")[:, 0:CC * O].rearrange("p (c n) -> p c n", c=CC)

        bank = [ctx.enter_context(nc.psum_tensor(f"bank{i}", [P, 512], F32)) for i in range(8)]
        halves = [b[:].rearrange("p (c n) -> p c n", c=2) for b in bank]

        names = """x_loaded xr_loaded small_loaded wl_loaded wg_loaded wv_loaded wo_loaded mask_loaded stored
            consts_set mask_cut top0 top0_all top1 top1_all topv topv_all scales0 scales1 scalev setup_a
            wk_rep_done setup_d setup_p wm_hi_done wk_hi_done wl_hi_done wvo_hi_done wm_lo_done wk_lo_done wl_lo_done
            wvo_lo_done wvo_mm sig_a sig_d
            x_hi_done x_lo_done wx_mm xw_hi_done xw_lo_done q_mm k_mm q_part_done q_max_done q_rel_done uv_done
            t_done ab_done vb_done att_done att_hi_done att_lo_done ot_mm den_done agg_done to_mm relu_done
            y_done y_stat_done y_mv_done y_var_done y_rstd_done h_done ht_mm ht_hi_done ht_lo_done
            z_mm z_hi_done z_lo_done s_mm sq_l_done sq_lc_done r_l_done diag_g_done diag_r_done g_mm clamp_done
            exp_done v_mm v_hi_done v_lo_done r_mm mr_done al_done dl_done sl_done ag_done dgr_done sg_done
            kl_done k_done kt_mm kt_hi_done kt_lo_done o_mm o_done o_stat_done o_mv_done o_var_done o_rstd_done
            normed""".split()
        s = {n: sem(n) for n in names}

        block = ctx.enter_context(nc.Block())

        def pipeline(engine, step):
            step(-2, False, False, True)
            step(-1, False, True, True)
            step(0, True, True, True)
            with engine.Fori(1, PAIRS - 2) as p:
                step(p, True, True, True)
            step(PAIRS - 2, True, True, False)
            step(PAIRS - 1, True, False, False)

        @block.sync
        def _(sp):
            sp.dma_start(adjT_raw, adjT.rearrange("(c p) o -> p c o", p=P)).then_inc(s["small_loaded"], 16)
            sp.dma_start(qk_raw[:, 0, :], wq).then_inc(s["small_loaded"], 16)
            sp.dma_start(qk_raw[:, 1, :], wk).then_inc(s["small_loaded"], 16)
            sp.dma_start(bias_m[:], bm).then_inc(s["small_loaded"], 16)
            sp.dma_start(knobs[:, 0:1], gate).then_inc(s["small_loaded"], 16)
            sp.dma_start(knobs[:, 1:2], sigma).then_inc(s["small_loaded"], 16)

            def step(p, l1, l0, new):
                q, r = p + 1, p + 2
                if l0:
                    wait(sp, s["y_done"], 4 * q)
                    wait(sp, s["x_loaded"], 16 * (q + 1))
                    sp.dma_start(x_res[:], x_in[:]).then_inc(s["xr_loaded"], 16)
                if new:
                    wait(sp, s["x_lo_done"], 2 * r)
                    wait(sp, s["xr_loaded"], 16 * r)
                    sp.dma_start(x_in[:], x_v[r]).then_inc(s["x_loaded"], 16)
                if isinstance(p, int) and p == -2:
                    sp.dma_start(mask[:], adj.rearrange("(c p) m -> p c m", p=P)).then_inc(s["mask_loaded"], 16)
                    sp.dma_start(wv_raw, wv.rearrange("(c p) d -> p c d", p=P)).then_inc(s["wv_loaded"], 16)
                    sp.dma_start(wo_raw, woT.rearrange("(c p) e -> p c e", p=P)).then_inc(s["wo_loaded"], 16)
                    sp.dma_start(wl_raw, wlT.rearrange("(c p) e -> p c e", p=P)).then_inc(s["wl_loaded"], 16)
                    sp.dma_start(wg_raw, wgT.rearrange("(c p) e -> p c e", p=P)).then_inc(s["wg_loaded"], 16)
                if l1:
                    for j in range(2):
                        sp.wait_ge(s["normed"], 2 * p + j + 1)
                        sp.dma_start(out_v[p, j], o[:, 2 * j:2 * j + 2, :]).then_inc(s["stored"], 16)

            pipeline(sp, step)
            sp.wait_ge(s["stored"], 32 * PAIRS)

        @block.tensor
        def _(pe):
            def product(dst, parts, skip=False, first=True):
                n = len(parts)
                for i, (ah, al, bh, bl) in enumerate(parts):
                    pe.matmul(dst, ah, bh, start=(i == 0 and first), stop=False, skip_group_check=skip)
                    pe.matmul(dst, ah, bl, start=False, stop=False, skip_group_check=skip)
                    last = pe.matmul(dst, al, bh, start=False, stop=(i == n - 1), skip_group_check=skip)
                return last

            def fuse_weights():
                pe.wait_ge(s["wv_loaded"], 16)
                pe.wait_ge(s["wo_loaded"], 16)
                for d in range(DC):
                    for f in range(DC):
                        last = pe.matmul(bank[d][:], wv_raw[:, f, d * P:(d + 1) * P], wo_raw[:, f, :],
                                         start=(f == 0), stop=(f == DC - 1))
                    last.then_inc(s["wvo_mm"], 1)

            def step(p, l1, l0, new):
                q, r = p + 1, p + 2
                if l1:
                    for g in range(8):
                        hi, lo = (wl_hi, wl_lo) if g < 4 else (wg_hi, wg_lo)
                        e = slice((g % 4) * P, (g % 4 + 1) * P)
                        if g == 0:
                            if isinstance(p, int) and p == 0:
                                pe.wait_ge(s["wl_lo_done"], 2)
                                pe.wait_ge(s["wvo_lo_done"], 4)
                            pe.wait_ge(s["ht_lo_done"], 4 * p + 4)
                        if g >= 4:
                            pe.wait_ge(s["z_lo_done"], 8 * p + g - 3)
                        product(bank[g % 4][:], [(hi[:, d, e], lo[:, d, e], ht_hi[:, d, :], ht_lo[:, d, :])
                                                 for d in range(DC)]).then_inc(s["z_mm"], 1)
                    for k in range(4):
                        kind, j = k // 2, k % 2
                        pe.wait_ge(s["z_lo_done"], 8 * p + 4 * kind + 4)
                        if k == 0:
                            wait(pe, s["q_rel_done"], p + 2 if new else PAIRS)
                            wait(pe, s["t_done"], 2 * p + 4 if new else 2 * PAIRS)
                            wait(pe, s["xw_lo_done"], 4 * p + 8 if new else 4 * PAIRS)
                        for c in range(OC):
                            rows = slice(j * O + c * P, j * O + (c + 1) * P)
                            cols = slice(j * O, (j + 1) * O)
                            last = product(halves[4 + k][:, c, :],
                                           [(z_hi[:, 4 * kind + e, rows], z_lo[:, 4 * kind + e, rows],
                                             z_hi[:, 4 * kind + e, cols], z_lo[:, 4 * kind + e, cols])
                                            for e in range(DC)], skip=True, first=(c == 0))
                        last.then_inc(s["s_mm"], 1)

                    def v_product(k):
                        rows = slice(k * P, (k + 1) * P)
                        pe_last = product(bank[k][:], [(ht_hi[:, d, rows], ht_lo[:, d, rows],
                                                        wvo_hi[:, d, :], wvo_lo[:, d, :]) for d in range(DC)])
                        pe_last.then_inc(s["v_mm"], 1)

                    v_product(0)
                    v_product(1)
                    for j in range(2):
                        pe.wait_ge(s["diag_g_done"], 2 * p + j + 1)
                        for c in range(OC):
                            last = pe.matmul(halves[6 + j][:, c, :], neg_ones[:], diag_g[:, j, :],
                                             start=False, stop=True, skip_group_check=True)
                        last.then_inc(s["g_mm"], 1)
                    v_product(2)
                    v_product(3)
                    pe.wait_ge(s["diag_r_done"], p + 1)
                    pe.wait_ge(s["v_lo_done"], 4 * p + 1)
                    pe.matmul(bank[0][:], ones[:], diag_r[:].rearrange("p a n -> p (a n)"),
                              start=True, stop=True).then_inc(s["r_mm"], 1)
                if l0:
                    if isinstance(p, int) and p == -1:
                        pe.wait_ge(s["wvo_lo_done"], 4)
                    for k in range(8):
                        j, m = k // NC, slice((k % NC) * P, (k % NC + 1) * P)
                        b = (1, 2, 3, 0)[k % 4]
                        pe.wait_ge(s["att_lo_done"], 8 * q + 4 * j + 4)
                        if k == 0:
                            pe.wait_ge(s["xw_lo_done"], 4 * q + 4)
                        if k < 3:
                            wait(pe, s["v_lo_done"], 4 * p + k + 2)
                        elif k == 3:
                            wait(pe, s["mr_done"], 2 * p + 2)
                        else:
                            pe.wait_ge(s["agg_done"], 8 * q + k - 3)
                        product(bank[b][:, 0:O + 1], [(att_hi[:, j, n, m], att_lo[:, j, n, m],
                                                       xw_hi[:, j, n, 0:O + 1], xw_lo[:, j, n, 0:O + 1])
                                                      for n in range(NC)]).then_inc(s["ot_mm"], 1)
                if l1:
                    for j in range(2):
                        pe.wait_ge(s["k_done"], 2 * p + j + 1)
                        for c in range(OC):
                            for m in range(OC):
                                last = pe.transpose(halves[4 + j][:, m, c * P:(c + 1) * P],
                                                    a_l[:, j, c, m * P:(m + 1) * P], ident[:])
                        last.then_inc(s["kt_mm"], 1)
                    for k in range(4):
                        j, c = k // 2, slice((k % 2) * P, (k % 2 + 1) * P)
                        pe.wait_ge(s["kt_lo_done"], 2 * p + j + 1)
                        if k == 0:
                            pe.wait_ge(s["v_lo_done"], 4 * p + 4)
                        if k >= 2:
                            pe.wait_ge(s["o_done"], 4 * p + k - 1)
                        product(bank[6 + k % 2][:], [(kt_hi[:, j, m, c], kt_lo[:, j, m, c],
                                                      v_hi[:, 2 * j + m, :], v_lo[:, 2 * j + m, :])
                                                     for m in range(OC)]).then_inc(s["o_mm"], 1)
                if l0:
                    pe.wait_ge(s["agg_done"], 8 * q + 8)
                    for k in range(4):
                        j, c = k // 2, slice((k % 2) * P, (k % 2 + 1) * P)
                        for m in range(NC):
                            last = pe.transpose(bank[(k + 1) % 4][:, m * P:(m + 1) * P], agg_t[:, j, m, c], ident[:])
                        last.then_inc(s["to_mm"], 1)
                if new:
                    for k in range(4):
                        j = k // 2
                        if k == 0:
                            if isinstance(p, int) and p == -2:
                                pe.wait_ge(s["wm_lo_done"], 1)
                        if k % 2 == 0:
                            pe.wait_ge(s["x_lo_done"], 2 * r + j + 1)
                        if k < 2:
                            wait(pe, s["kt_lo_done"], 2 * p + k + 1)
                        else:
                            wait(pe, s["o_done"], 4 * p + k + 1)
                        for i in range(2):
                            n = slice((2 * (k % 2) + i) * P, (2 * (k % 2) + i + 1) * P)
                            last = product(halves[4 + k][:, i, :],
                                           [(x_hi[:, j, c, n], x_lo[:, j, c, n], wm_hi[:, c, :], wm_lo[:, c, :])
                                            for c in range(CC)])
                        last.then_inc(s["wx_mm"], 1)
                if isinstance(p, int) and p == -2:
                    fuse_weights()
                if l0:
                    pe.wait_ge(s["h_done"], 4 * q + 4)
                    for d in range(DC):
                        for k in range(4):
                            last = pe.transpose(bank[d][:, k * P:(k + 1) * P], h[:, k, d * P:(d + 1) * P], ident[:])
                        last.then_inc(s["ht_mm"], 1)
                if new:
                    if isinstance(p, int) and p == -2:
                        pe.wait_ge(s["wk_lo_done"], 1)
                    pe.wait_ge(s["xw_lo_done"], 4 * r + 1)
                    for j in range(2):
                        for n in range(NC):
                            cols = slice(n * P, (n + 1) * P)
                            last = product(bank[4][:, j * NC + n:j * NC + n + 1],
                                           [(x_hi[:, j, c, cols], x_lo[:, j, c, cols], wq_hi[:, c, :], wq_lo[:, c, :])
                                            for c in range(CC)])
                    last.then_inc(s["q_mm"], 1)
                    for j in range(2):
                        pe.wait_ge(s["xw_lo_done"], 4 * r + 2 + j)
                        product(bank[5 + j][:], [(wk_hi[:, c, :], wk_lo[:, c, :], x_hi[:, j, c, :], x_lo[:, j, c, :])
                                                 for c in range(CC)]).then_inc(s["k_mm"], 1)

            pe.wait_ge(s["consts_set"], 5)
            pe.wait_ge(s["setup_p"], 5)
            pipeline(pe, step)

        @block.scalar
        def _(act):
            def split_setup0():
                act.wait_ge(s["scales0"], 1)
                act.activation(wm_hi[:], adjT_raw, ACT.Copy, scale=scale[:, 0:1]).then_inc(s["wm_hi_done"], 1)
                act.activation(wq_hi[:, :, 0], qk_raw[:, 0, :], ACT.Copy, scale=scale[:, 1:2])
                act.wait_ge(s["wk_rep_done"], 1)
                act.activation(wk_hi[:], wk_rep[:], ACT.Copy, scale=scale[:, 1:2]).then_inc(s["wk_hi_done"], 1)
                act.activation(tiny[:, 0:1], knobs[:, 0:1], ACT.Exp, scale=-1.0)
                act.activation(tiny[:, 1:2], knobs[:, 1:2], ACT.Exp, scale=-2.0).then_inc(s["sig_a"], 1)

            def split_setup1():
                act.wait_ge(s["scales1"], 1)
                act.activation(wl_hi[:], wl_raw, ACT.Copy, scale=scale[:, 2:3]).then_inc(s["wl_hi_done"], 1)
                act.activation(wg_hi[:], wg_raw, ACT.Copy, scale=scale[:, 3:4]).then_inc(s["wl_hi_done"], 1)
                act.wait_ge(s["scalev"], 1)
                for d in range(DC):
                    act.activation(wvo_hi[:, d, :], bank[d][:], ACT.Copy, scale=scale[:, 4:5])\
                       .then_inc(s["wvo_hi_done"], 1)

            def step(p, l1, l0, new):
                q, r = p + 1, p + 2

                def vb_tile(g):
                    j, n = g // NC, g % NC
                    act.wait_ge(s["ab_done"], 2 * q + j + 1)
                    act.wait_ge(s["uv_done"], q + 1)
                    wait(act, s["att_done"], 8 * q + g - 1)
                    act.activation(vb[:, g % 2, :], b_row[:, j, :], ACT.Copy, scale=v_col[:, j, n:n + 1])\
                       .then_inc(s["vb_done"], 1)

                def att_hi_tile(g):
                    wait(act, s["ot_mm"], 8 * q)
                    act.wait_ge(s["att_done"], 8 * q + g + 1)
                    act.activation(att_hi[:, g // NC, g % NC, :], att[:, g % 2, :], ACT.Copy)\
                       .then_inc(s["att_hi_done"], 1)

                for g in range(8):
                    if l0:
                        vb_tile(g)
                    if l1:
                        act.wait_ge(s["z_mm"], 8 * p + g + 1)
                        act.activation(z_hi[:, g, :], bank[g % 4][:], ACT.Copy).then_inc(s["z_hi_done"], 1)
                    if l0 and g >= 1:
                        att_hi_tile(g - 1)
                if l0:
                    att_hi_tile(7)
                if l1:
                    for k in range(4):
                        act.wait_ge(s["v_mm"], 4 * p + k + 1)
                        act.activation(v_hi[:, k, :], bank[k][:], ACT.Copy).then_inc(s["v_hi_done"], 1)
                    for j in range(2):
                        act.wait_ge(s["clamp_done"], 2 * p + j + 1)
                        act.activation(a_g[:, j], a_g[:, j], ACT.Exp, scale=c_grav[:, 0:1]).then_inc(s["exp_done"], 1)
                if l0:
                    for k in range(8):
                        act.wait_ge(s["den_done"], 8 * q + k + 1)
                        act.activation(agg_t[:, k // NC, k % NC, :], bank[(1, 2, 3, 0)[k % 4]][:, 0:O], ACT.Copy,
                                       scale=den_inv[:, k:k + 1]).then_inc(s["agg_done"], 1)
                if l1:
                    for j in range(2):
                        act.wait_ge(s["kt_mm"], 2 * p + j + 1)
                        act.activation(kt_hi[:, j], halves[4 + j], ACT.Copy).then_inc(s["kt_hi_done"], 1)
                if l0:
                    wait(act, s["h_done"], 4 * q)
                    for k in range(4):
                        act.wait_ge(s["to_mm"], 4 * q + k + 1)
                        act.activation(y[:, k, :], bank[(k + 1) % 4][:], ACT.Relu, bias=bias_m[:, k % 2:k % 2 + 1],
                                       scale=unscale[:, 0:1]).then_inc(s["relu_done"], 1)
                if new:
                    for k in range(4):
                        act.wait_ge(s["wx_mm"], 4 * r + k + 1)
                        act.activation(xw_hi[:, k // 2, 2 * (k % 2):2 * (k % 2) + 2, 0:O], halves[4 + k], ACT.Copy)\
                           .then_inc(s["xw_hi_done"], 1)
                if isinstance(p, int) and p == -2:
                    split_setup1()
                if l0:
                    for d in range(DC):
                        act.wait_ge(s["ht_mm"], 4 * q + d + 1)
                        act.activation(ht_hi[:, d, :], bank[d][:], ACT.Copy).then_inc(s["ht_hi_done"], 1)
                if new:
                    act.wait_ge(s["q_rel_done"], r + 1)
                    wait(act, s["att_done"], 8 * r)
                    wait(act, s["vb_done"], 8 * r)
                    act.activation(u_col[:], q_rel[:], ACT.Exp, scale=c_u[:, 0:1])
                    act.activation(v_col[:], q_rel[:], ACT.Exp, scale=c_v[:, 0:1]).then_inc(s["uv_done"], 1)
                    for j in range(2):
                        act.wait_ge(s["t_done"], 2 * r + j + 1)
                        act.activation(a_row[:, j, :], a_row[:, j, :], ACT.Exp, bias=shift[:, 0:1], scale=c_a[:, 0:1])
                        act.activation(b_row[:, j, :], b_row[:, j, :], ACT.Exp, bias=shift[:, 0:1], scale=c_b[:, 0:1])\
                           .then_inc(s["ab_done"], 1)

            split_setup0()
            act.wait_ge(s["setup_d"], 1)
            act.wait_ge(s["consts_set"], 5)
            pipeline(act, step)

        @block.vector
        def _(dve):
            def scales(cols, ready, done, count):
                lo, hi = cols
                dve.wait_ge(ready, 1)
                dve.tensor_scalar(unscale[:, lo:hi], top_all[:, lo:hi], 1e-30, 1.0 / TOP, ALU.max, ALU.mult)\
                   .then_inc(s["setup_a"], 1)
                dve.wait_ge(s["setup_a"], count)
                dve.reciprocal(scale[:, lo:hi], unscale[:, lo:hi]).then_inc(done, 1)

            def setup0():
                dve.memset(ones[:], 1.0).then_inc(s["consts_set"], 1)
                dve.memset(neg_ones[:], -1.0).then_inc(s["consts_set"], 1)
                dve.memset(xw_hi[:, :, :, O:OW], 1.0).then_inc(s["consts_set"], 1)
                dve.memset(xw_lo[:, :, :, O:OW], 0.0).then_inc(s["consts_set"], 1)
                dve.memset(shift[:], LN256).then_inc(s["consts_set"], 1)
                dve.wait_ge(s["small_loaded"], 96)
                dve.tensor_reduce(top_part[:, 0:1], adjT_raw, AX.XY, ALU.max, apply_absolute_value=True)
                dve.tensor_reduce(top_part[:, 1:2], qk_raw[:], AX.XY, ALU.max, apply_absolute_value=True)\
                   .then_inc(s["top0"], 1)
                dve.wait_ge(s["consts_set"], 5)
                for c in range(CC):
                    last = dve.tensor_scalar(wk_rep[:, c, :], ones[:], qk_raw[:, 1, c:c + 1], None, ALU.mult)
                last.then_inc(s["wk_rep_done"], 1)
                scales((0, 2), s["top0_all"], s["scales0"], 1)
                dve.wait_ge(s["wm_hi_done"], 1)
                dve.wait_ge(s["scales0"], 1)
                dve.scalar_tensor_tensor(out=wm_lo[:], in0=adjT_raw, scalar=scale[:, 0:1], in1=wm_hi[:],
                                         op0=ALU.mult, op1=ALU.subtract).then_inc(s["wm_lo_done"], 1)
                dve.wait_ge(s["wk_hi_done"], 1)
                dve.scalar_tensor_tensor(out=wq_lo[:, :, 0], in0=qk_raw[:, 0, :], scalar=scale[:, 1:2],
                                         in1=wq_hi[:, :, 0], op0=ALU.mult, op1=ALU.subtract)
                dve.scalar_tensor_tensor(out=wk_lo[:], in0=wk_rep[:], scalar=scale[:, 1:2], in1=wk_hi[:],
                                         op0=ALU.mult, op1=ALU.subtract).then_inc(s["wk_lo_done"], 1)
                dve.tensor_scalar(c_u[:], unscale[:, 1:2], 1.0, None, ALU.mult)
                dve.tensor_scalar(c_v[:], unscale[:, 1:2], SLOPE, None, ALU.mult)
                dve.tensor_scalar(c_a[:], unscale[:, 1:2], 1.0 - SLOPE, None, ALU.mult)
                dve.tensor_scalar(c_b[:], unscale[:, 1:2], SLOPE - 1.0, None, ALU.mult).then_inc(s["setup_d"], 1)

            def setup1():
                dve.wait_ge(s["wl_loaded"], 16)
                dve.tensor_reduce(top_part[:, 2:3], wl_raw, AX.XY, ALU.max, apply_absolute_value=True)
                dve.wait_ge(s["wg_loaded"], 16)
                dve.tensor_reduce(top_part[:, 3:4], wg_raw, AX.XY, ALU.max, apply_absolute_value=True)\
                   .then_inc(s["top1"], 1)
                scales((2, 4), s["top1_all"], s["scales1"], 2)
                dve.wait_ge(s["wvo_mm"], DC)
                for d in range(DC):
                    last = dve.tensor_reduce(tiny[:, 2 + d:3 + d], bank[d][:], AX.X, ALU.max, apply_absolute_value=True)
                last.then_inc(s["sig_d"], 1)
                dve.wait_ge(s["sig_d"], 1)
                dve.tensor_reduce(top_part[:, 4:5], tiny[:, 2:2 + DC], AX.X, ALU.max).then_inc(s["topv"], 1)
                scales((4, 5), s["topv_all"], s["scalev"], 3)
                for i, (lo, hi, raw) in enumerate(((wl_lo, wl_hi, wl_raw), (wg_lo, wg_hi, wg_raw))):
                    dve.wait_ge(s["wl_hi_done"], i + 1)
                    dve.scalar_tensor_tensor(out=lo[:], in0=raw, scalar=scale[:, 2 + i:3 + i], in1=hi[:],
                                             op0=ALU.mult, op1=ALU.subtract).then_inc(s["wl_lo_done"], 1)
                dve.wait_ge(s["scalev"], 1)
                for d in range(DC):
                    dve.wait_ge(s["wvo_hi_done"], d + 1)
                    dve.scalar_tensor_tensor(out=wvo_lo[:, d, :], in0=bank[d][:], scalar=scale[:, 4:5],
                                             in1=wvo_hi[:, d, :], op0=ALU.mult, op1=ALU.subtract)\
                       .then_inc(s["wvo_lo_done"], 1)
                dve.wait_ge(s["sig_a"], 1)
                dve.tensor_scalar(tiny[:, 6:7], tiny[:, 0:1], 1.0, None, ALU.add).then_inc(s["sig_d"], 1)
                dve.wait_ge(s["sig_d"], 2)
                dve.reciprocal(tiny[:, 7:8], tiny[:, 6:7]).then_inc(s["sig_d"], 1)
                dve.wait_ge(s["sig_d"], 3)
                dve.tensor_scalar(c_wl[:], tiny[:, 7:8], 256.0, None, ALU.mult)
                dve.tensor_scalar(c_wg[:], tiny[:, 7:8], -256.0, 256.0, ALU.mult, ALU.add)
                dve.tensor_scalar(c_out[:], unscale[:, 4:5], 1.0 / 256.0, None, ALU.mult)
                dve.scalar_tensor_tensor(out=c_grav[:], in0=unscale[:, 3:4], scalar=unscale[:, 3:4],
                                         in1=tiny[:, 1:2], op0=ALU.mult, op1=ALU.mult)
                dve.scalar_tensor_tensor(out=tiny[:, 6:7], in0=scale[:, 2:3], scalar=NORM_EPS2,
                                         in1=scale[:, 2:3], op0=ALU.mult, op1=ALU.mult).then_inc(s["setup_d"], 1)
                dve.wait_ge(s["setup_d"], 2)
                dve.tensor_scalar(c_norm[:], ones[:, 0:4], tiny[:, 6:7], None, ALU.mult).then_inc(s["setup_d"], 1)
                dve.wait_ge(s["setup_d"], 3)

            def step(p, l1, l0, new):
                q, r = p + 1, p + 2

                def den(k):
                    if l0:
                        dve.wait_ge(s["ot_mm"], 8 * q + k + 1)
                        wait(dve, s["agg_done"], 8 * p + k + 1)
                        dve.reciprocal(den_inv[:, k:k + 1], bank[(1, 2, 3, 0)[k % 4]][:, O:O + 1])\
                           .then_inc(s["den_done"], 1)

                def v_lo_tile(k):
                    dve.wait_ge(s["v_hi_done"], 4 * p + k + 1)
                    dve.tensor_tensor(v_lo[:, k, :], bank[k][:], v_hi[:, k, :], ALU.subtract)\
                       .then_inc(s["v_lo_done"], 1)

                def xw_lo_tile(k):
                    if new:
                        dve.wait_ge(s["xw_hi_done"], 4 * r + k + 1)
                        n = slice(2 * (k % 2), 2 * (k % 2) + 2)
                        dve.tensor_tensor(xw_lo[:, k // 2, n, 0:O], halves[4 + k], xw_hi[:, k // 2, n, 0:O],
                                          ALU.subtract).then_inc(s["xw_lo_done"], 1)

                for g in range(8):
                    if l1:
                        dve.wait_ge(s["z_hi_done"], 8 * p + g + 1)
                        dve.tensor_tensor(z_lo[:, g, :], bank[g % 4][:], z_hi[:, g, :], ALU.subtract)\
                           .then_inc(s["z_lo_done"], 1)
                    if l0:
                        j, n = g // NC, g % NC
                        dve.wait_ge(s["vb_done"], 8 * q + g + 1)
                        wait(dve, s["att_lo_done"], 8 * q + g - 1)
                        dve.scalar_tensor_tensor(out=att[:, g % 2, :], in0=a_row[:, j, :],
                                                 scalar=u_col[:, j, n:n + 1], in1=vb[:, g % 2, :],
                                                 op0=ALU.mult, op1=ALU.max).then_inc(s["att_done"], 1)
                if new:
                    dve.wait_ge(s["x_loaded"], 16 * (r + 1))
                    wait(dve, s["k_mm"], 2 * r)
                    for j in range(2):
                        dve.tensor_copy(x_hi[:, j], x_in[:, j]).then_inc(s["x_hi_done"], 1)
                if l1:
                    for k in range(4):
                        j, c = k // 2, k % 2
                        dve.wait_ge(s["s_mm"], 4 * p + j + 1)
                        block_ = halves[4 + j][:, c, c * P:(c + 1) * P]
                        last = dve.scalar_tensor_tensor(out=diag_junk[:, k, :], in0=block_, scalar=1.0, in1=ident[:],
                                                        op0=ALU.mult, op1=ALU.mult, accum_out=sq_l[:, k:k + 1])
                    last.then_inc(s["sq_l_done"], 1)
                    dve.wait_ge(s["sq_l_done"], p + 1)
                    dve.tensor_scalar(sq_lc[:], sq_l[:], c_norm[:, 0:1], None, ALU.max).then_inc(s["sq_lc_done"], 1)
                    for k in range(4):
                        j, c = k // 2, k % 2
                        dve.wait_ge(s["s_mm"], 4 * p + 3 + j)
                        block_ = halves[6 + j][:, c, c * P:(c + 1) * P]
                        last = dve.scalar_tensor_tensor(out=diag_g[:, j, c * P:(c + 1) * P], in0=block_, scalar=0.5,
                                                        in1=ident[:], op0=ALU.mult, op1=ALU.mult,
                                                        accum_out=sq_g[:, k:k + 1])
                        if c == 1:
                            last.then_inc(s["diag_g_done"], 1)
                    dve.wait_ge(s["r_l_done"], p + 1)
                    for k in range(4):
                        last = dve.tensor_scalar(diag_r[:, k, :], ident[:], r_l[:, k:k + 1], None, ALU.mult)
                    last.then_inc(s["diag_r_done"], 1)
                    v_lo_tile(0)
                    v_lo_tile(1)
                    for j in range(2):
                        dve.wait_ge(s["g_mm"], 2 * p + j + 1)
                        dve.wait_ge(s["diag_g_done"], 2 * p + j + 1)
                        for c in range(OC):
                            last = dve.tensor_scalar(a_g[:, j, c, :], halves[6 + j][:, c, :],
                                                     sq_g[:, 2 * j + c:2 * j + c + 1], 0.0, ALU.subtract, ALU.min)
                        last.then_inc(s["clamp_done"], 1)
                    v_lo_tile(2)
                    v_lo_tile(3)
                    for j in range(2):
                        dve.wait_ge(s["r_mm"], p + 1)
                        for c in range(OC):
                            last = dve.tensor_tensor(a_l[:, j, c, :], halves[0][:, j, :], mask[:, c, :], ALU.mult)
                        last.then_inc(s["mr_done"], 1)
                    den(0)
                    for k in range(4):
                        j, c = k // 2, k % 2
                        dve.wait_ge(s["mr_done"], 2 * p + j + 1)
                        last = dve.scalar_tensor_tensor(out=a_l[:, j, c, :], in0=halves[4 + j][:, c, :], scalar=0.0,
                                                        in1=a_l[:, j, c, :], op0=ALU.max, op1=ALU.mult,
                                                        accum_out=deg_l[:, k:k + 1])
                        if k == 1:
                            den(1)
                    last.then_inc(s["al_done"], 1)
                    den(2)
                    for k in range(4):
                        j, c = k // 2, k % 2
                        dve.wait_ge(s["exp_done"], 2 * p + j + 1)
                        last = dve.scalar_tensor_tensor(out=a_g[:, j, c, :], in0=a_g[:, j, c, :], scalar=1.0,
                                                        in1=mask[:, c, :], op0=ALU.mult, op1=ALU.mult,
                                                        accum_out=deg_g[:, k:k + 1])
                    last.then_inc(s["ag_done"], 1)
                    den(3)
                    dve.wait_ge(s["al_done"], p + 1)
                    dve.tensor_tensor(deg_l2[:], deg_l[:], r_l[:], ALU.mult).then_inc(s["dl_done"], 1)
                    dve.wait_ge(s["ag_done"], p + 1)
                    dve.tensor_scalar(deg_g2[:], deg_g[:], DEG_EPS, None, ALU.max).then_inc(s["dgr_done"], 1)
                    dve.wait_ge(s["dl_done"], 3 * p + 1)
                    dve.tensor_scalar(deg_l3[:], deg_l2[:], DEG_EPS, None, ALU.max).then_inc(s["dl_done"], 1)
                    dve.wait_ge(s["dgr_done"], 2 * p + 1)
                    dve.reciprocal(deg_g3[:], deg_g2[:]).then_inc(s["dgr_done"], 1)
                    dve.wait_ge(s["dl_done"], 3 * p + 2)
                    dve.reciprocal(deg_l4[:], deg_l3[:]).then_inc(s["dl_done"], 1)
                    dve.wait_ge(s["dgr_done"], 2 * p + 2)
                    dve.tensor_scalar(s_g[:], deg_g3[:], c_wg[:, 0:1], None, ALU.mult).then_inc(s["sg_done"], 1)
                    dve.wait_ge(s["dl_done"], 3 * p + 3)
                    dve.scalar_tensor_tensor(out=s_l[:], in0=deg_l4[:], scalar=c_wl[:, 0:1], in1=r_l[:],
                                             op0=ALU.mult, op1=ALU.mult).then_inc(s["sl_done"], 1)
                    den(4)
                    dve.wait_ge(s["sl_done"], p + 1)
                    for k in range(4):
                        j, c = k // 2, k % 2
                        dve.tensor_scalar(a_l[:, j, c, :], a_l[:, j, c, :], s_l[:, k:k + 1], None, ALU.mult)\
                           .then_inc(s["kl_done"], 1)
                    dve.wait_ge(s["sg_done"], p + 1)
                    for k in range(4):
                        j, c = k // 2, k % 2
                        dve.wait_ge(s["kl_done"], 4 * p + k + 1)
                        last = dve.scalar_tensor_tensor(out=a_l[:, j, c, :], in0=a_g[:, j, c, :],
                                                        scalar=s_g[:, k:k + 1], in1=a_l[:, j, c, :],
                                                        op0=ALU.mult, op1=ALU.add)
                        if c == 1:
                            last.then_inc(s["k_done"], 1)
                            den(5 + j)
                    den(7)
                    for j in range(2):
                        dve.wait_ge(s["kt_hi_done"], 2 * p + j + 1)
                        dve.tensor_tensor(kt_lo[:, j], halves[4 + j], kt_hi[:, j], ALU.subtract)\
                           .then_inc(s["kt_lo_done"], 1)
                    wait(dve, s["stored"], 32 * p)
                    for k in range(4):
                        dve.wait_ge(s["o_mm"], 4 * p + k + 1)
                        dve.scalar_tensor_tensor(out=o[:, k, :], in0=bank[6 + k % 2][:], scalar=c_out[:, 0:1],
                                                 in1=h[:, k, :], op0=ALU.mult, op1=ALU.add).then_inc(s["o_done"], 1)
                else:
                    for k in range(8):
                        den(k)
                if l0:
                    def y_stat_tile(k):
                        dve.wait_ge(s["y_done"], 4 * q + k + 1)
                        dve.bn_stats(y_stat[:, k, :], y[:, k, :]).then_inc(s["y_stat_done"], 1)

                    dve.wait_ge(s["xr_loaded"], 16 * (q + 1))
                    for k in range(4):
                        dve.wait_ge(s["relu_done"], 4 * q + k + 1)
                        dve.tensor_tensor(y[:, k, :], y[:, k, :], x_res[:, k // 2, k % 2, :], ALU.add)\
                           .then_inc(s["y_done"], 1)
                        if k >= 1:
                            y_stat_tile(k - 1)
                    y_stat_tile(3)
                    wait(dve, s["y_rstd_done"], q)
                    dve.wait_ge(s["y_stat_done"], 4 * q + 4)
                    dve.tensor_scalar(turn_y[:], y_stat[:, 3, 0:1], 1.0, None, ALU.mult)
                    for k in range(4):
                        last = dve.bn_aggr(y_mv[:, k, :], y_stat[:, k, :])
                    last.then_inc(s["y_mv_done"], 1)
                xw_lo_tile(0)
                xw_lo_tile(1)
                if l0:
                    dve.wait_ge(s["y_rstd_done"], q + 1)
                    dve.wait_ge(s["y_mv_done"], q + 1)
                    for k in range(4):
                        dve.tensor_scalar(h[:, k, :], y[:, k, :], y_mv[:, k, 0:1], y_rstd[:, k:k + 1],
                                          ALU.subtract, ALU.mult).then_inc(s["h_done"], 1)
                xw_lo_tile(2)
                xw_lo_tile(3)
                if isinstance(p, int) and p == -2:
                    setup1()
                if l0:
                    for d in range(DC):
                        dve.wait_ge(s["ht_hi_done"], 4 * q + d + 1)
                        dve.tensor_tensor(ht_lo[:, d, :], bank[d][:], ht_hi[:, d, :], ALU.subtract)\
                           .then_inc(s["ht_lo_done"], 1)
                if new:
                    dve.wait_ge(s["q_mm"], r + 1)
                    q_psum = bank[4][:, 0:2 * NC].rearrange("p (j n) -> p j n", j=2)
                    dve.tensor_reduce(q_part[:], q_psum, AX.X, ALU.max).then_inc(s["q_part_done"], 1)
                    dve.wait_ge(s["q_max_done"], r + 1)
                    wait(dve, s["uv_done"], r)
                    for j in range(2):
                        last = dve.tensor_scalar(q_rel[:, j, :], q_psum[:, j, :], q_max[:, j:j + 1], None, ALU.subtract)
                    last.then_inc(s["q_rel_done"], 1)
                    for j in range(2):
                        dve.wait_ge(s["k_mm"], 2 * r + j + 1)
                        dve.tensor_scalar(a_row[:, j, :], bank[5 + j][:], q_max[:, j:j + 1], 0.0, ALU.add, ALU.min)
                        dve.tensor_scalar(b_row[:, j, :], bank[5 + j][:], q_max[:, j:j + 1], 0.0, ALU.add, ALU.max)\
                           .then_inc(s["t_done"], 1)
                if l1:
                    wait(dve, s["o_rstd_done"], p)
                    for k in range(4):
                        dve.wait_ge(s["o_done"], 4 * p + k + 1)
                        dve.bn_stats(o_stat[:, k, :], o[:, k, :]).then_inc(s["o_stat_done"], 1)
                    dve.wait_ge(s["o_stat_done"], 4 * p + 4)
                    dve.tensor_scalar(turn_o[:], o_stat[:, 3, 0:1], 1.0, None, ALU.mult)
                    for k in range(4):
                        last = dve.bn_aggr(o_mv[:, k, :], o_stat[:, k, :])
                    last.then_inc(s["o_mv_done"], 1)
                    dve.wait_ge(s["o_rstd_done"], p + 1)
                    dve.wait_ge(s["o_mv_done"], p + 1)
                    for k in range(4):
                        last = dve.tensor_scalar(o[:, k, :], o[:, k, :], o_mv[:, k, 0:1], o_rstd[:, k:k + 1],
                                                 ALU.subtract, ALU.mult)
                        if k % 2 == 1:
                            last.then_inc(s["normed"], 1)

            setup0()
            pipeline(dve, step)

        @block.gpsimd
        def _(pool):
            pool.memset(ident[:], 0.0).then_inc(s["setup_p"], 1)
            pool.memset(exponent[:], -0.5).then_inc(s["setup_p"], 1)
            pool.memset(top_part[:, 5:8], 0.0).then_inc(s["setup_p"], 1)
            pool.memset(eps[:], LN_EPS).then_inc(s["setup_p"], 1)
            pool.wait_ge(s["setup_p"], 4)
            pool.affine_select(out=ident[:], in_=ident[:], compare_op=ALU.not_equal, fill=1.0, base=0,
                               pattern=[[-1, P]], channel_multiplier=1).then_inc(s["setup_p"], 1)

            def largest(cols, ready, done):
                pool.wait_ge(ready, 1)
                pool.partition_all_reduce(top_all[:, cols[0]:cols[1]], top_part[:, cols[0]:cols[1]], P, RMAX)\
                    .then_inc(done, 1)

            def setup1():
                pool.wait_ge(s["mask_loaded"], 16)
                pool.affine_select(out=mask[:], in_=mask[:], compare_op=ALU.not_equal, fill=0.0, base=0,
                                   pattern=[[P, OC], [-1, O]], channel_multiplier=1).then_inc(s["mask_cut"], 1)
                largest((2, 4), s["top1"], s["top1_all"])
                largest((4, 5), s["topv"], s["topv_all"])

            def step(p, l1, l0, new):
                q, r = p + 1, p + 2
                if l0:
                    wait(pool, s["ot_mm"], 8 * q)
                    for g in range(8):
                        pool.wait_ge(s["att_hi_done"], 8 * q + g + 1)
                        n = (g // NC, g % NC)
                        pool.tensor_tensor(att_lo[:, n[0], n[1], :], att[:, g % 2, :], att_hi[:, n[0], n[1], :],
                                           ALU.subtract).then_inc(s["att_lo_done"], 1)
                if l1:
                    pool.wait_ge(s["sq_lc_done"], p + 1)
                    wait(pool, s["sl_done"], p)
                    pool.tensor_tensor(r_l[:], sq_lc[:], exponent[:], ALU.pow).then_inc(s["r_l_done"], 1)
                if new:
                    wait(pool, s["k_mm"], 2 * r)
                    for j in range(2):
                        pool.wait_ge(s["x_hi_done"], 2 * r + j + 1)
                        pool.tensor_tensor(x_lo[:, j], x_in[:, j], x_hi[:, j], ALU.subtract)\
                            .then_inc(s["x_lo_done"], 1)
                if l0:
                    pool.wait_ge(s["y_mv_done"], q + 1)
                    pool.tensor_tensor(y_var[:], y_mv[:, :, 1], eps[:], ALU.add).then_inc(s["y_var_done"], 1)
                    pool.wait_ge(s["y_var_done"], q + 1)
                    wait(pool, s["h_done"], 4 * q)
                    pool.tensor_tensor(y_rstd[:], y_var[:], exponent[:], ALU.pow).then_inc(s["y_rstd_done"], 1)
                if isinstance(p, int) and p == -2:
                    setup1()
                if new:
                    pool.wait_ge(s["q_part_done"], r + 1)
                    pool.tensor_tensor(turn_q[:], q_part[:], q_part[:], ALU.add)
                    pool.partition_all_reduce(q_max[:], q_part[:], P, RMAX).then_inc(s["q_max_done"], 1)
                if l1:
                    pool.wait_ge(s["o_mv_done"], p + 1)
                    pool.tensor_tensor(o_var[:], o_mv[:, :, 1], eps[:], ALU.add).then_inc(s["o_var_done"], 1)
                    pool.wait_ge(s["o_var_done"], p + 1)
                    wait(pool, s["normed"], 2 * p)
                    pool.tensor_tensor(o_rstd[:], o_var[:], exponent[:], ALU.pow).then_inc(s["o_rstd_done"], 1)

            largest((0, 2), s["top0"], s["top0_all"])
            pipeline(pool, step)


_SHAPE = (32, 256, 512)


def kernel(**inputs):
    import numpy as np
    import concourse.bacc as bacc
    from concourse.bass_utils import run_bass_kernel_spmd

    a = {k: np.asarray(v) for k, v in inputs.items()}
    laid = {
        "x": a["x"],
        "adj": a["adj"],
        "adjT": a["adj"].T,
        "wq": a["L0_gnn_wq"].reshape(2, P).T,
        "wk": a["L0_gnn_wk"].reshape(2, P).T,
        "bm": a["L0_gnn_bm"].reshape(2, P).T,
        "wlT": a["L1_gnn_W_lang"].T,
        "wgT": a["L1_gnn_W_grav"].T,
        "wv": a["L1_gnn_W_V"],
        "woT": a["L1_gnn_W_O"].T,
        "gate": np.broadcast_to(a["L1_gnn_gate_logit"].reshape(1, 1), (P, 1)),
        "sigma": np.broadcast_to(a["L1_gnn_log_sigma"].reshape(1, 1), (P, 1)),
    }
    nc = bacc.Bacc("TRN2", target_bir_lowering=False, num_devices=1)
    arrays, args = {}, []
    for name, v in laid.items():
        v = np.ascontiguousarray(v)
        arrays[f"in_{name}"] = v
        args.append(nc.dram_tensor(f"in_{name}", v.shape, mybir.dt.from_np(v.dtype), kind="ExternalInput").ap())
    args.append(nc.dram_tensor("out_y", _SHAPE, F32, kind="ExternalOutput").ap())
    build(nc, *args)
    r = run_bass_kernel_spmd(nc, [arrays], core_ids=[0])
    return r.results[0]["out_y"]
```

```python
from contextlib import ExitStack

import concourse.bass as bass
from concourse import mybir

F32 = mybir.dt.float32
F16 = mybir.dt.float16
ALU = mybir.AluOpType
ACT = mybir.ActivationFunctionType
AX = mybir.AxisListType
RMAX = bass.bass_isa.ReduceOp.max

P = 128
LN_EPS = 1e-5
DEG_EPS = 1e-8
NORM_EPS2 = 1e-16
SLOPE = 0.01
TOP = 4.0
LN256 = 5.545177444479562


def wait(engine, semaphore, count):
    if not (isinstance(count, int) and count <= 0):
        engine.wait_ge(semaphore, count)


def build(nc, x, adj, adjT, wqk, bm, wl, wg, wv, woT, gate, sigma, out):
    B, C, N = x.shape
    O = adj.shape[0]
    D = wl.shape[0]
    PAIRS = B // 2
    CC, OC, NC, DC = C // P, O // P, N // P, D // P
    assert C == O == 2 * P and N == D == 4 * P

    x_v = x.rearrange("(t j) (c p) n -> t p j c n", j=2, p=P)
    out_v = out.rearrange("(t j) (c p) n -> t j p c n", j=2, p=P)

    with ExitStack() as ctx:
        def sb(name, shape, dt=F32):
            return ctx.enter_context(nc.sbuf_tensor(name, [P, *shape], dt))

        def sem(name):
            return ctx.enter_context(nc.semaphore(name))

        ident = sb("ident", [P])
        ones = sb("ones", [P])
        ident16, ones16 = sb("ident16", [P], F16), sb("ones16", [P], F16)
        neg16 = sb("neg16", [P], F16)
        mask = sb("mask", [OC, O])
        exponent = sb("exponent", [4])
        shift = sb("shift", [1])
        bias_m = sb("bias_m", [OC])
        ul_hi, ul_lo = sb("ul_hi", [DC, D], F16), sb("ul_lo", [DC, D], F16)
        ug_hi, ug_lo = sb("ug_hi", [DC, D], F16), sb("ug_lo", [DC, D], F16)
        wvo_hi, wvo_lo = sb("wvo_hi", [DC, D], F16), sb("wvo_lo", [DC, D], F16)
        OW = O + 2
        wm_hi, wm_lo = sb("wm_hi", [CC, OW], F16), sb("wm_lo", [CC, OW], F16)
        qk_raw = sb("qk_raw", [CC, 2])
        knobs = sb("knobs", [2])
        top_part, top_all = sb("top_part", [8]), sb("top_all", [8])
        scale = sb("scale", [8])
        unscale = sb("unscale", [8])
        half_scale = sb("half_scale", [2])
        top_gram = sb("top_gram", [2, 3])
        c_u, c_v, c_a, c_b = (sb(n, [1]) for n in ("c_u", "c_v", "c_a", "c_b"))
        c_grav, c_wl, c_wg, c_out = (sb(n, [1]) for n in ("c_grav", "c_wl", "c_wg", "c_out"))
        c_norm = sb("c_norm", [4])
        tiny = sb("tiny", [8])
        eps = sb("eps", [4])
        turn_q, turn_y, turn_o = sb("turn_q", [2]), sb("turn_y", [1]), sb("turn_o", [1])
        x_in = sb("x_in", [2, CC, N])
        x_res = sb("x_res", [2, CC, N])
        x_hi, x_lo = sb("x_hi", [2, CC, N], F16), sb("x_lo", [2, CC, N], F16)
        xw_hi, xw_lo = sb("xw_hi", [2, NC, OW], F16), sb("xw_lo", [2, NC, OW], F16)
        qk = sb("qk", [2 * NC, 2])
        q_part, q_max, q_rel = sb("q_part", [2]), sb("q_max", [2]), sb("q_rel", [2, NC])
        q_cols = qk[:, :, 0].rearrange("p (j n) -> p j n", j=2)
        k_hi, k_lo = sb("k_hi", [2 * NC], F16), sb("k_lo", [2 * NC], F16)
        dk_hi, dk_lo = sb("dk_hi", [2 * NC, P], F16), sb("dk_lo", [2 * NC, P], F16)
        u_col, v_col = sb("u_col", [2, NC]), sb("v_col", [2, NC])
        a_row, b_row = sb("a_row", [2, N]), sb("b_row", [2, N])
        vb = sb("vb", [2, N])
        att = sb("att", [2, N])
        att_hi, att_lo = sb("att_hi", [2, NC, N], F16), sb("att_lo", [2, NC, N], F16)
        den_inv = sb("den_inv", [8])
        agg_t = sb("agg_t", [2, NC, O])
        y = sb("y", [2 * OC, N])
        y_stat, y_mv = sb("y_stat", [2 * OC, 6]), sb("y_mv", [2 * OC, 2])
        y_var, y_rstd = sb("y_var", [2 * OC]), sb("y_rstd", [2 * OC])
        h = sb("h", [2 * OC, N])
        ht_hi, ht_lo = sb("ht_hi", [DC, 2 * O], F16), sb("ht_lo", [DC, 2 * O], F16)
        z_hi, z_lo = sb("z_hi", [2 * DC, 2 * O], F16), sb("z_lo", [2 * DC, 2 * O], F16)
        v_hi, v_lo = sb("v_hi", [2 * OC, D], F16), sb("v_lo", [2 * OC, D], F16)
        diag_junk = sb("diag_junk", [8, P])
        sq_l, sq_lc, r_l = sb("sq_l", [4]), sb("sq_lc", [4]), sb("r_l", [4])
        sq_g, sq_ghi, sq_glo = sb("sq_g", [4]), sb("sq_ghi", [4], F16), sb("sq_glo", [4], F16)
        diag_ghi, diag_glo = sb("diag_ghi", [2, O], F16), sb("diag_glo", [2, O], F16)
        diag_r = sb("diag_r", [4, P])
        a_l, a_g = sb("a_l", [2, OC, O]), sb("a_g", [2, OC, O])
        deg_l, deg_l2, deg_l3, deg_l4, s_l = (sb(n, [4]) for n in ("deg_l", "deg_l2", "deg_l3", "deg_l4", "s_l"))
        deg_g, deg_g2, deg_g3, s_g = (sb(n, [4]) for n in ("deg_g", "deg_g2", "deg_g3", "s_g"))
        kt_hi, kt_lo = sb("kt_hi", [2, OC, O], F16), sb("kt_lo", [2, OC, O], F16)
        o = sb("o", [2 * OC, N])
        o_stat, o_mv = sb("o_stat", [2 * OC, 6]), sb("o_mv", [2 * OC, 2])
        o_var, o_rstd = sb("o_var", [2 * OC]), sb("o_rstd", [2 * OC])
        wl_raw = agg_t[:].rearrange("p j c n -> p (j c n)").rearrange("p (c n) -> p c n", c=DC)
        wg_raw, wv_raw, wo_raw = y[:], o[:], h[:]
        adjT_raw = att[:].rearrange("p a n -> p (a n)")[:, 0:CC * O].rearrange("p (c n) -> p c n", c=CC)

        bank = [ctx.enter_context(nc.psum_tensor(f"bank{i}", [P, 512], F32)) for i in range(8)]
        halves = [b[:].rearrange("p (c n) -> p c n", c=2) for b in bank]

        wvo_bank = (7, 4, 5, 6)
        gram_rows = (((0, 0, 0), (1, 1, 0), (3, 1, 3 * P), (2, 2, 0)),
                     ((0, 3, 0), (1, 6, 0), (3, 6, 3 * P), (2, 2, 2 * P)))
        v_bank = (0, 1, 2, 7)
        late = (6, 7, 4, 5)
        names = """x_loaded xr_loaded small_loaded wl_loaded wg_loaded wv_loaded wo_loaded mask_loaded stored
            consts_set mask_cut top0 top0_all top_l top_l_all top_g top_g_all topv topv_all scales0 scales_l scales_g scalev half_l half_g gram_mm gram_part u_hi_done u_lo_done setup_a
            setup_d setup_p wm_hi_done wqk_hi_done wvo_hi_done wm_lo_done wqk_lo_done 
            wvo_lo_done wvo_mm sig_a sig_d
            x_hi_done x_lo_done wx_mm xw_hi_done xw_lo_done k_mm k_hi_done k_lo_done dk_done q_part_done q_max_done q_rel_done uv_done
            t_done ab_done vb_done att_done att_hi_done att_lo_done ot_mm den_done agg_done to_mm relu_done
            y_done y_odd_done y_stat_done y_mv_done y_var_done y_rstd_done h_done ht_mm ht_hi_done ht_lo_done
            z_mm z_hi_done z_lo_done t_mm tcopy_done s_mm sq_l_done sq_lc_done r_l_done sq_g_done sq_ghi_done sq_glo_done diag_g_done diag_r_done g_mm clamp_done
            exp_done v_mm v_hi_done v_lo_done r_mm mr_done al_done dl_done sl_done ag_done dgr_done sg_done
            kl_done k_done kt_mm kt_hi_done kt_lo_done o_mm o_done o_stat_done o_mv_done o_var_done o_rstd_done
            normed""".split()
        s = {n: sem(n) for n in names}

        block = ctx.enter_context(nc.Block())

        def pipeline(engine, step):
            step(-2, False, False, True)
            step(-1, False, True, True)
            step(0, True, True, True)
            with engine.Fori(1, PAIRS - 2) as p:
                step(p, True, True, True)
            step(PAIRS - 2, True, True, False)
            step(PAIRS - 1, True, False, False)

        @block.sync
        def _(sp):
            sp.dma_start(adjT_raw, adjT.rearrange("(c p) o -> p c o", p=P)).then_inc(s["small_loaded"], 16)
            sp.dma_start(qk_raw[:], wqk).then_inc(s["small_loaded"], 16)
            sp.dma_start(bias_m[:], bm).then_inc(s["small_loaded"], 16)
            sp.dma_start(knobs[:, 0:1], gate).then_inc(s["small_loaded"], 16)
            sp.dma_start(knobs[:, 1:2], sigma).then_inc(s["small_loaded"], 16)

            def step(p, l1, l0, new):
                q, r = p + 1, p + 2
                if l0:
                    wait(sp, s["y_done"], 2 * q)
                    wait(sp, s["y_odd_done"], 2 * q)
                    wait(sp, s["x_loaded"], 16 * (q + 1))
                    sp.dma_start(x_res[:], x_in[:]).then_inc(s["xr_loaded"], 16)
                if new:
                    wait(sp, s["x_lo_done"], 2 * r)
                    wait(sp, s["xr_loaded"], 16 * r)
                    sp.dma_start(x_in[:], x_v[r]).then_inc(s["x_loaded"], 16)
                if isinstance(p, int) and p == -2:
                    sp.dma_start(wl_raw, wl.rearrange("(c p) d -> p c d", p=P)).then_inc(s["wl_loaded"], 16)
                    sp.dma_start(wg_raw, wg.rearrange("(c p) d -> p c d", p=P)).then_inc(s["wg_loaded"], 16)
                    sp.dma_start(wv_raw, wv.rearrange("(c p) d -> p c d", p=P)).then_inc(s["wv_loaded"], 16)
                    sp.dma_start(wo_raw, woT.rearrange("(c p) e -> p c e", p=P)).then_inc(s["wo_loaded"], 16)
                    sp.dma_start(mask[:], adj.rearrange("(c p) m -> p c m", p=P)).then_inc(s["mask_loaded"], 16)
                if l1:
                    for j in range(2):
                        sp.wait_ge(s["normed"], 2 * p + j + 1)
                        sp.dma_start(out_v[p, j], o[:, 2 * j:2 * j + 2, :]).then_inc(s["stored"], 16)

            pipeline(sp, step)
            sp.wait_ge(s["stored"], 32 * PAIRS)

        @block.tensor
        def _(pe):
            def product(dst, parts, skip=False, first=True):
                n = len(parts)
                for i, (ah, al, bh, bl) in enumerate(parts):
                    pe.matmul(dst, ah, bh, start=(i == 0 and first), stop=False, skip_group_check=skip)
                    pe.matmul(dst, ah, bl, start=False, stop=False, skip_group_check=skip)
                    last = pe.matmul(dst, al, bh, start=False, stop=(i == n - 1), skip_group_check=skip)
                return last

            def gram(kind):
                raw = (wl_raw, wg_raw)[kind]
                pe.wait_ge(s[("wl_loaded", "wg_loaded")[kind]], 16)
                for i, (d, b, col) in enumerate(gram_rows[kind]):
                    width = D - d * P
                    if kind == 1 and i == 1:
                        pe.wait_ge(s["xw_lo_done"], 8)
                    if kind == 1 and i == 3:
                        pe.wait_ge(s["u_lo_done"], 1)
                    for f in range(DC):
                        last = pe.matmul(bank[b][:, col:col + width], raw[:, f, d * P:(d + 1) * P],
                                         raw[:, f, d * P:D], start=(f == 0 and i != 2),
                                         stop=(f == DC - 1), skip_group_check=True)
                last.then_inc(s["gram_mm"], 1)

            def fuse_weights():
                pe.wait_ge(s["wv_loaded"], 16)
                pe.wait_ge(s["wo_loaded"], 16)
                pe.wait_ge(s["t_done"], 2)
                for d in range(DC):
                    if d == DC - 1:
                        pe.wait_ge(s["u_lo_done"], 2)
                    for f in range(DC):
                        last = pe.matmul(bank[wvo_bank[d]][:], wv_raw[:, f, d * P:(d + 1) * P], wo_raw[:, f, :],
                                         start=(f == 0), stop=(f == DC - 1))
                    last.then_inc(s["wvo_mm"], 1)

            def step(p, l1, l0, new):
                q, r = p + 1, p + 2
                def k_rows():
                    pe.wait_ge(s["dk_done"], q + 1)
                    for j, b in ((0, 7), (1, 4)):
                        pe.wait_ge(s["xw_lo_done"], 8 * q + 8)
                        n = slice(j * NC, (j + 1) * NC)
                        pe.matmul(bank[b][:], ones16[:], dk_hi[:, n, :].rearrange("p a n -> p (a n)"),
                                  start=True, stop=False)
                        pe.matmul(bank[b][:], ones16[:], dk_lo[:, n, :].rearrange("p a n -> p (a n)"),
                                  start=False, stop=True).then_inc(s["k_mm"], 1)

                if l0 and not l1:
                    k_rows()
                    gram(1)
                    fuse_weights()
                if l1:
                    for g in range(8):
                        hi, lo = (ul_hi, ul_lo) if g < 4 else (ug_hi, ug_lo)
                        block_e = DC - 1 - g % 4
                        e = slice(block_e * P, (block_e + 1) * P)
                        if g == 0:
                            pe.wait_ge(s["ht_lo_done"], 4 * p + 4)
                        if g >= 4:
                            pe.wait_ge(s["z_lo_done"], 8 * p + g - 3)
                        product(bank[g % 4][:], [(hi[:, d, e], lo[:, d, e], ht_hi[:, d, :], ht_lo[:, d, :])
                                                 for d in range(block_e + 1)]).then_inc(s["z_mm"], 1)
                        if g == 1 and l0:
                            k_rows()

                    def t_product(k):
                        kind, j = k // 2, k % 2
                        pe.wait_ge(s["z_lo_done"], 8 * p + 4 * kind + 4)
                        if k == 0:
                            if l0:
                                pe.wait_ge(s["t_done"], 2 * q + 2)
                                pe.wait_ge(s["xw_lo_done"], 8 * q + 8)
                            else:
                                pe.wait_ge(s["o_done"], 4 * p)
                        cols = slice(j * O, (j + 1) * O)
                        for c in range(OC):
                            rows = slice(j * O + c * P, j * O + (c + 1) * P)
                            last = product(halves[4 + k][:, c, :],
                                           [(z_hi[:, 4 * kind + g, rows], z_lo[:, 4 * kind + g, rows],
                                             ht_hi[:, DC - 1 - g, cols], ht_lo[:, DC - 1 - g, cols])
                                            for g in range(DC)], skip=True, first=(c == 0))
                        last.then_inc(s["t_mm"], 1)

                    def add_transposed(k):
                        kind, j = k // 2, k % 2
                        t_copy = (a_l, a_g)[kind]
                        pe.wait_ge(s["tcopy_done"], 4 * p + k + 1)
                        for c in range(OC):
                            for m in range(OC):
                                last = pe.matmul(halves[4 + k][:, c, m * P:(m + 1) * P],
                                                 t_copy[:, j, m, c * P:(c + 1) * P], ident[:],
                                                 start=False, stop=True, skip_group_check=True)
                        last.then_inc(s["s_mm"], 1)

                    t_product(0)
                    t_product(1)
                    t_product(2)
                    t_product(3)
                    add_transposed(0)
                    add_transposed(1)

                    if isinstance(p, int) and p == 0:
                        pe.wait_ge(s["wvo_lo_done"], 4)

                    def v_product(k):
                        rows = slice(k * P, (k + 1) * P)
                        pe_last = product(bank[v_bank[k]][:], [(ht_hi[:, d, rows], ht_lo[:, d, rows],
                                                        wvo_hi[:, d, :], wvo_lo[:, d, :]) for d in range(DC)])
                        pe_last.then_inc(s["v_mm"], 1)

                    v_product(0)
                    add_transposed(2)
                    add_transposed(3)
                    v_product(1)
                    v_product(2)
                    for j in range(2):
                        pe.wait_ge(s["diag_g_done"], 2 * p + j + 1)
                        for c in range(OC):
                            pe.matmul(halves[6 + j][:, c, :], neg16[:], diag_ghi[:, j, :],
                                      start=False, stop=False, skip_group_check=True)
                            last = pe.matmul(halves[6 + j][:, c, :], neg16[:], diag_glo[:, j, :],
                                             start=False, stop=True, skip_group_check=True)
                        last.then_inc(s["g_mm"], 1)
                    pe.wait_ge(s["diag_r_done"], p + 1)
                    pe.wait_ge(s["v_lo_done"], 4 * p + 1)
                    pe.matmul(bank[0][:], ones[:], diag_r[:].rearrange("p a n -> p (a n)"),
                              start=True, stop=True).then_inc(s["r_mm"], 1)
                if l0:
                    for k in range(8):
                        j, m = k // NC, slice((k % NC) * P, (k % NC + 1) * P)
                        b = (1, 2, 3, 0)[k % 4]
                        pe.wait_ge(s["att_lo_done"], 8 * q + 4 * j + 4)
                        if k == 0:
                            pe.wait_ge(s["xw_lo_done"], 8 * q + 8)
                        if k < 2:
                            wait(pe, s["v_lo_done"], 4 * p + k + 2)
                        elif k == 3:
                            wait(pe, s["mr_done"], 2 * p + 2)
                        elif k >= 4:
                            pe.wait_ge(s["agg_done"], 8 * q + k - 3)
                        product(bank[b][:, 0:O + 1], [(att_hi[:, j, n, m], att_lo[:, j, n, m],
                                                       xw_hi[:, j, n, 0:O + 1], xw_lo[:, j, n, 0:O + 1])
                                                      for n in range(NC)]).then_inc(s["ot_mm"], 1)
                if l1:
                    for j in range(2):
                        pe.wait_ge(s["k_done"], 2 * p + j + 1)
                        for c in range(OC):
                            for m in range(OC):
                                last = pe.transpose(halves[4 + j][:, m, c * P:(c + 1) * P],
                                                    a_l[:, j, c, m * P:(m + 1) * P], ident[:])
                        last.then_inc(s["kt_mm"], 1)
                if l0:
                    pe.wait_ge(s["agg_done"], 8 * q + 8)
                    for k in range(4):
                        j, c = k // 2, slice((k % 2) * P, (k % 2 + 1) * P)
                        for m in range(NC):
                            last = pe.transpose(bank[(k + 1) % 4][:, m * P:(m + 1) * P], agg_t[:, j, m, c], ident[:])
                        last.then_inc(s["to_mm"], 1)
                if l1:
                    pe.wait_ge(s["clamp_done"], 2 * p + 2)
                    v_product(3)
                    for k in range(4):
                        j, c = k // 2, slice((k % 2) * P, (k % 2 + 1) * P)
                        pe.wait_ge(s["kt_lo_done"], 2 * p + j + 1)
                        if k == 0:
                            pe.wait_ge(s["v_lo_done"], 4 * p + 2)
                        if k == 1:
                            pe.wait_ge(s["v_lo_done"], 4 * p + 4)
                        product(bank[late[k]][:], [(kt_hi[:, j, m, c], kt_lo[:, j, m, c],
                                                      v_hi[:, 2 * j + m, :], v_lo[:, 2 * j + m, :])
                                                     for m in range(OC)]).then_inc(s["o_mm"], 1)
                def wx_product(k):
                    j, n = k // NC, slice((k % NC) * P, (k % NC + 1) * P)
                    if isinstance(p, int) and p == -1 and k < 4:
                        pe.wait_ge(s["wvo_lo_done"], 4)
                    if k % 4 == 0:
                        pe.wait_ge(s["x_lo_done"], 2 * r + j + 1)
                    if k < 4:
                        wait(pe, s["o_done"], 4 * p + k + 1)
                    else:
                        pe.wait_ge(s["xw_lo_done"], 8 * r + k - 3)
                    product(bank[late[k % 4]][:, 0:OW],
                            [(x_hi[:, j, c, n], x_lo[:, j, c, n], wm_hi[:, c, :], wm_lo[:, c, :])
                             for c in range(CC)]).then_inc(s["wx_mm"], 1)

                if new:
                    if isinstance(p, int) and p == -2:
                        pe.wait_ge(s["wm_lo_done"], 1)
                        pe.wait_ge(s["wqk_lo_done"], 1)
                    for k in range(4):
                        wx_product(k)
                if l0:
                    pe.wait_ge(s["h_done"], 4 * q + 4)
                    for d in range(DC):
                        for k in range(4):
                            last = pe.transpose(bank[d][:, k * P:(k + 1) * P], h[:, k, d * P:(d + 1) * P], ident[:])
                        last.then_inc(s["ht_mm"], 1)
                if new:
                    for k in range(4, 8):
                        wx_product(k)
                if isinstance(p, int) and p == -2:
                    gram(0)

            pe.wait_ge(s["consts_set"], 7)
            pe.wait_ge(s["setup_p"], 5)
            pipeline(pe, step)

        @block.scalar
        def _(act):
            def split_setup0():
                act.wait_ge(s["scales0"], 1)
                act.activation(wm_hi[:, :, 0:O], adjT_raw, ACT.Copy, scale=scale[:, 0:1]).then_inc(s["wm_hi_done"], 1)
                act.activation(wm_hi[:, :, O:OW], qk_raw[:], ACT.Copy, scale=scale[:, 1:2]).then_inc(s["wqk_hi_done"], 1)
                act.activation(tiny[:, 0:1], knobs[:, 0:1], ACT.Exp, scale=-1.0)
                act.activation(tiny[:, 1:2], knobs[:, 1:2], ACT.Exp, scale=-2.0).then_inc(s["sig_a"], 1)

            def u_hi(kind):
                act.wait_ge(s[("half_l", "half_g")[kind]], 1)
                hi = (ul_hi, ug_hi)[kind]
                for d, b, col in gram_rows[kind]:
                    last = act.activation(hi[:, d, d * P:(d + 1) * P], bank[b][:, col:col + P], ACT.Copy,
                                          scale=half_scale[:, kind:kind + 1])
                    if d < DC - 1:
                        last = act.activation(hi[:, d, (d + 1) * P:D], bank[b][:, col + P:col + D - d * P], ACT.Copy,
                                              scale=scale[:, 2 + kind:3 + kind])
                last.then_inc(s["u_hi_done"], 1)

            def wvo_hi_tile(d):
                act.wait_ge(s["scalev"], 1)
                act.activation(wvo_hi[:, d, :], bank[wvo_bank[d]][:], ACT.Copy, scale=scale[:, 4:5])\
                   .then_inc(s["wvo_hi_done"], 1)

            def step(p, l1, l0, new):
                q, r = p + 1, p + 2

                def vb_tile(g):
                    j, n = g // NC, g % NC
                    act.wait_ge(s["ab_done"], 2 * q + j + 1)
                    act.wait_ge(s["uv_done"], q + 1)
                    wait(act, s["att_done"], 8 * q + g - 1)
                    act.activation(vb[:, g % 2, :], b_row[:, j, :], ACT.Copy, scale=v_col[:, j, n:n + 1])\
                       .then_inc(s["vb_done"], 1)

                def att_hi_tile(g):
                    wait(act, s["ot_mm"], 8 * q)
                    act.wait_ge(s["att_done"], 8 * q + g + 1)
                    act.activation(att_hi[:, g // NC, g % NC, :], att[:, g % 2, :], ACT.Copy)\
                       .then_inc(s["att_hi_done"], 1)

                def ab_rows():
                    for j in range(2):
                        act.wait_ge(s["t_done"], 2 * q + j + 1)
                        act.activation(a_row[:, j, :], a_row[:, j, :], ACT.Exp, bias=shift[:, 0:1], scale=c_a[:, 0:1])
                        act.activation(b_row[:, j, :], b_row[:, j, :], ACT.Exp, bias=shift[:, 0:1], scale=c_b[:, 0:1])\
                           .then_inc(s["ab_done"], 1)

                def t_copy(k):
                    act.wait_ge(s["t_mm"], 4 * p + k + 1)
                    act.activation((a_l, a_g)[k // 2][:, k % 2], halves[4 + k], ACT.Copy).then_inc(s["tcopy_done"], 1)

                def v_hi_tile(k):
                    act.wait_ge(s["v_mm"], 4 * p + k + 1)
                    act.activation(v_hi[:, k, :], bank[v_bank[k]][:], ACT.Copy).then_inc(s["v_hi_done"], 1)

                for g in range(8 + 6):
                    if l1 and g < 8:
                        act.wait_ge(s["z_mm"], 8 * p + g + 1)
                        act.activation(z_hi[:, g, :], bank[g % 4][:], ACT.Copy).then_inc(s["z_hi_done"], 1)
                    if l0 and g == 4:
                        ab_rows()
                    if l0 and 5 <= g < 13:
                        vb_tile(g - 5)
                    if l0 and g >= 6:
                        att_hi_tile(g - 6)
                    if l1 and g in (9, 11, 13):
                        t_copy((g - 9) // 2)
                    if isinstance(p, int) and p == -1 and g == 8:
                        u_hi(1)
                if l1:
                    t_copy(3)
                    for k in range(3):
                        v_hi_tile(k)
                    for j in range(2):
                        act.wait_ge(s["clamp_done"], 2 * p + j + 1)
                        act.activation(a_g[:, j], a_g[:, j], ACT.Exp, scale=c_grav[:, 0:1]).then_inc(s["exp_done"], 1)
                if l0:
                    for k in range(8):
                        act.wait_ge(s["den_done"], 8 * q + k + 1)
                        act.activation(agg_t[:, k // NC, k % NC, :], bank[(1, 2, 3, 0)[k % 4]][:, 0:O], ACT.Copy,
                                       scale=den_inv[:, k:k + 1]).then_inc(s["agg_done"], 1)
                        if k >= 4 and isinstance(p, int) and p == -1:
                            wvo_hi_tile(k - 4)
                if l1:
                    for j in range(2):
                        act.wait_ge(s["kt_mm"], 2 * p + j + 1)
                        act.activation(kt_hi[:, j], halves[4 + j], ACT.Copy).then_inc(s["kt_hi_done"], 1)
                if l0:
                    wait(act, s["h_done"], 4 * q)
                    for k in range(4):
                        act.wait_ge(s["to_mm"], 4 * q + k + 1)
                        act.activation(y[:, k, :], bank[(k + 1) % 4][:], ACT.Relu, bias=bias_m[:, k % 2:k % 2 + 1],
                                       scale=unscale[:, 0:1]).then_inc(s["relu_done"], 1)
                if l1:
                    v_hi_tile(3)
                def xw_hi_tile(k):
                    act.wait_ge(s["wx_mm"], 8 * r + k + 1)
                    act.activation(xw_hi[:, k // NC, k % NC, 0:O], bank[late[k % 4]][:, 0:O], ACT.Copy)\
                       .then_inc(s["xw_hi_done"], 1)

                if new:
                    for k in range(4):
                        xw_hi_tile(k)
                if l0:
                    for d in range(DC):
                        act.wait_ge(s["ht_mm"], 4 * q + d + 1)
                        act.activation(ht_hi[:, d, :], bank[d][:], ACT.Copy).then_inc(s["ht_hi_done"], 1)
                if new:
                    for k in range(4, 8):
                        xw_hi_tile(k)
                if new:
                    act.wait_ge(s["q_rel_done"], r + 1)
                    wait(act, s["att_done"], 8 * r)
                    wait(act, s["vb_done"], 8 * r)
                    act.activation(u_col[:], q_rel[:], ACT.Exp, scale=c_u[:, 0:1])
                    act.activation(v_col[:], q_rel[:], ACT.Exp, scale=c_v[:, 0:1]).then_inc(s["uv_done"], 1)
                if isinstance(p, int) and p == -2:
                    u_hi(0)

            split_setup0()
            act.wait_ge(s["setup_d"], 1)
            act.wait_ge(s["consts_set"], 7)
            pipeline(act, step)

        @block.vector
        def _(dve):
            def scales(cols, ready, done, count):
                lo, hi = cols
                dve.wait_ge(ready, 1)
                dve.tensor_scalar(unscale[:, lo:hi], top_all[:, lo:hi], 1e-30, 1.0 / TOP, ALU.max, ALU.mult)\
                   .then_inc(s["setup_a"], 1)
                dve.wait_ge(s["setup_a"], count)
                dve.reciprocal(scale[:, lo:hi], unscale[:, lo:hi]).then_inc(done, 1)

            def setup0():
                dve.memset(ones[:], 1.0).then_inc(s["consts_set"], 1)
                dve.memset(ones16[:], 1.0).then_inc(s["consts_set"], 1)
                dve.memset(neg16[:], -16.0).then_inc(s["consts_set"], 1)
                dve.wait_ge(s["setup_p"], 5)
                dve.tensor_copy(ident16[:], ident[:]).then_inc(s["consts_set"], 1)
                dve.memset(xw_hi[:, :, :, O:OW], 1.0).then_inc(s["consts_set"], 1)
                dve.memset(xw_lo[:, :, :, O:OW], 0.0).then_inc(s["consts_set"], 1)
                dve.memset(shift[:], LN256).then_inc(s["consts_set"], 1)
                dve.wait_ge(s["small_loaded"], 80)
                dve.tensor_reduce(top_part[:, 0:1], adjT_raw, AX.XY, ALU.max, apply_absolute_value=True)
                dve.tensor_reduce(top_part[:, 1:2], qk_raw[:], AX.XY, ALU.max, apply_absolute_value=True)\
                   .then_inc(s["top0"], 1)
                dve.wait_ge(s["consts_set"], 7)
                scales((0, 2), s["top0_all"], s["scales0"], 1)
                dve.wait_ge(s["wm_hi_done"], 1)
                dve.wait_ge(s["scales0"], 1)
                dve.scalar_tensor_tensor(out=wm_lo[:, :, 0:O], in0=adjT_raw, scalar=scale[:, 0:1], in1=wm_hi[:, :, 0:O],
                                         op0=ALU.mult, op1=ALU.subtract).then_inc(s["wm_lo_done"], 1)
                dve.wait_ge(s["wqk_hi_done"], 1)
                dve.scalar_tensor_tensor(out=wm_lo[:, :, O:OW], in0=qk_raw[:], scalar=scale[:, 1:2], in1=wm_hi[:, :, O:OW],
                                         op0=ALU.mult, op1=ALU.subtract).then_inc(s["wqk_lo_done"], 1)
                dve.tensor_scalar(c_u[:], unscale[:, 1:2], 1.0, None, ALU.mult)
                dve.tensor_scalar(c_v[:], unscale[:, 1:2], SLOPE, None, ALU.mult)
                dve.tensor_scalar(c_a[:], unscale[:, 1:2], 1.0 - SLOPE, None, ALU.mult)
                dve.tensor_scalar(c_b[:], unscale[:, 1:2], SLOPE - 1.0, None, ALU.mult).then_inc(s["setup_d"], 1)

            def gram_top(kind):
                dve.wait_ge(s["gram_mm"], kind + 1)
                for i, (b, lo, hi) in enumerate((((0, 0, D), (1, 0, D), (2, 0, 2 * P)),
                                                 ((3, 0, D), (6, 0, D), (2, 2 * P, D)))[kind]):
                    last = dve.tensor_reduce(top_gram[:, kind, i:i + 1], bank[b][:, lo:hi], AX.X, ALU.max,
                                             apply_absolute_value=True)
                last.then_inc(s["gram_part"], 1)
                dve.wait_ge(s["gram_part"], kind + 1)
                dve.tensor_reduce(top_part[:, 2 + kind:3 + kind], top_gram[:, kind, :], AX.X, ALU.max)\
                   .then_inc(s[("top_l", "top_g")[kind]], 1)

            def gram_scales(kind):
                ready, done, half = (("top_l_all", "scales_l", "half_l"), ("top_g_all", "scales_g", "half_g"))[kind]
                scales((2 + kind, 3 + kind), s[ready], s[done], 2 + kind)
                dve.wait_ge(s[done], 1)
                dve.tensor_scalar(half_scale[:, kind:kind + 1], scale[:, 2 + kind:3 + kind], 0.5, None, ALU.mult)\
                   .then_inc(s[half], 1)

            def u_lo(kind):
                dve.wait_ge(s["u_hi_done"], kind + 1)
                dve.wait_ge(s[("half_l", "half_g")[kind]], 1)
                hi, lo = ((ul_hi, ul_lo), (ug_hi, ug_lo))[kind]
                for d, b, col in gram_rows[kind]:
                    own, rest = slice(d * P, (d + 1) * P), slice((d + 1) * P, D)
                    last = dve.scalar_tensor_tensor(out=lo[:, d, own], in0=bank[b][:, col:col + P],
                                                    scalar=half_scale[:, kind:kind + 1], in1=hi[:, d, own],
                                                    op0=ALU.mult, op1=ALU.subtract)
                    if d < DC - 1:
                        last = dve.scalar_tensor_tensor(out=lo[:, d, rest], in0=bank[b][:, col + P:col + D - d * P],
                                                        scalar=scale[:, 2 + kind:3 + kind], in1=hi[:, d, rest],
                                                        op0=ALU.mult, op1=ALU.subtract)
                last.then_inc(s["u_lo_done"], 1)

            def split_wvo(k):
                if k < 4:
                    dve.wait_ge(s["wvo_mm"], k + 1)
                    dve.tensor_reduce(tiny[:, 2 + k:3 + k], bank[wvo_bank[k]][:], AX.X, ALU.max,
                                      apply_absolute_value=True).then_inc(s["sig_d"], 1)
                elif k == 4:
                    dve.wait_ge(s["sig_d"], 4)
                    dve.tensor_reduce(top_part[:, 4:5], tiny[:, 2:2 + DC], AX.X, ALU.max).then_inc(s["topv"], 1)
                    scales((4, 5), s["topv_all"], s["scalev"], 4)
                for d in {5: (0,), 6: (1,), 7: (2, 3)}.get(k, ()):
                    dve.wait_ge(s["wvo_hi_done"], d + 1)
                    dve.scalar_tensor_tensor(out=wvo_lo[:, d, :], in0=bank[wvo_bank[d]][:], scalar=scale[:, 4:5],
                                             in1=wvo_hi[:, d, :], op0=ALU.mult, op1=ALU.subtract)\
                       .then_inc(s["wvo_lo_done"], 1)

            def constants():
                dve.wait_ge(s["sig_a"], 1)
                dve.tensor_scalar(tiny[:, 6:7], tiny[:, 0:1], 1.0, None, ALU.add).then_inc(s["sig_d"], 1)
                dve.wait_ge(s["sig_d"], 5)
                dve.reciprocal(tiny[:, 7:8], tiny[:, 6:7]).then_inc(s["sig_d"], 1)
                dve.wait_ge(s["sig_d"], 6)
                dve.tensor_scalar(c_wl[:], tiny[:, 7:8], 256.0, None, ALU.mult)
                dve.tensor_scalar(c_wg[:], tiny[:, 7:8], -256.0, 256.0, ALU.mult, ALU.add)
                dve.tensor_scalar(c_out[:], unscale[:, 4:5], 1.0 / 256.0, None, ALU.mult)
                dve.tensor_scalar(c_grav[:], tiny[:, 1:2], unscale[:, 3:4], None, ALU.mult)
                dve.tensor_scalar(tiny[:, 6:7], scale[:, 2:3], NORM_EPS2, None, ALU.mult).then_inc(s["setup_d"], 1)
                dve.wait_ge(s["setup_d"], 2)
                dve.tensor_scalar(c_norm[:], ones[:, 0:4], tiny[:, 6:7], None, ALU.mult).then_inc(s["setup_d"], 1)
                dve.wait_ge(s["setup_d"], 3)
                dve.wait_ge(s["mask_cut"], 1)

            def o_stat_tiles(pair, half):
                for k in (2 * half, 2 * half + 1):
                    dve.wait_ge(s["o_done"], 4 * pair + k + 1)
                    dve.bn_stats(o_stat[:, k, :], o[:, k, :]).then_inc(s["o_stat_done"], 1)

            def o_mean(pair):
                dve.wait_ge(s["o_stat_done"], 4 * pair + 4)
                dve.tensor_scalar(turn_o[:], o_stat[:, 3, 0:1], 1.0, None, ALU.mult)
                for k in range(4):
                    last = dve.bn_aggr(o_mv[:, k, :], o_stat[:, k, :])
                last.then_inc(s["o_mv_done"], 1)

            def o_norm(pair):
                dve.wait_ge(s["o_rstd_done"], pair + 1)
                dve.wait_ge(s["o_mv_done"], pair + 1)
                for k in range(4):
                    last = dve.tensor_scalar(o[:, k, :], o[:, k, :], o_mv[:, k, 0:1], o_rstd[:, k:k + 1],
                                             ALU.subtract, ALU.mult)
                    if k % 2 == 1:
                        last.then_inc(s["normed"], 1)

            def step(p, l1, l0, new):
                q, r = p + 1, p + 2

                def den(k):
                    dve.wait_ge(s["ot_mm"], 8 * q + k + 1)
                    wait(dve, s["agg_done"], 8 * p + k + 1)
                    dve.reciprocal(den_inv[:, k:k + 1], bank[(1, 2, 3, 0)[k % 4]][:, O:O + 1])\
                       .then_inc(s["den_done"], 1)

                def v_lo_tile(k):
                    dve.wait_ge(s["v_hi_done"], 4 * p + k + 1)
                    dve.tensor_tensor(v_lo[:, k, :], bank[v_bank[k]][:], v_hi[:, k, :], ALU.subtract)\
                       .then_inc(s["v_lo_done"], 1)

                def xw_lo_tile(k):
                    dve.wait_ge(s["xw_hi_done"], 8 * r + k + 1)
                    dve.tensor_copy(qk[:, k, :], bank[late[k % 4]][:, O:OW])
                    dve.tensor_tensor(xw_lo[:, k // NC, k % NC, 0:O], bank[late[k % 4]][:, 0:O],
                                      xw_hi[:, k // NC, k % NC, 0:O], ALU.subtract).then_inc(s["xw_lo_done"], 1)

                def t_rows():
                    for j, b in ((0, 7), (1, 4)):
                        dve.wait_ge(s["k_mm"], 2 * q + j + 1)
                        dve.tensor_scalar(a_row[:, j, :], bank[b][:], q_max[:, j:j + 1], 0.0, ALU.add, ALU.min)
                        dve.tensor_scalar(b_row[:, j, :], bank[b][:], q_max[:, j:j + 1], 0.0, ALU.add, ALU.max)\
                           .then_inc(s["t_done"], 1)

                def att_tile(g):
                    j, n = g // NC, g % NC
                    dve.wait_ge(s["vb_done"], 8 * q + g + 1)
                    wait(dve, s["att_lo_done"], 8 * q + g - 1)
                    dve.scalar_tensor_tensor(out=att[:, g % 2, :], in0=a_row[:, j, :], scalar=u_col[:, j, n:n + 1],
                                             in1=vb[:, g % 2, :], op0=ALU.mult, op1=ALU.max)\
                       .then_inc(s["att_done"], 1)

                for g in range(8 + 5):
                    if l1 and g < 8:
                        dve.wait_ge(s["z_hi_done"], 8 * p + g + 1)
                        dve.tensor_tensor(z_lo[:, g, :], bank[g % 4][:], z_hi[:, g, :], ALU.subtract)\
                           .then_inc(s["z_lo_done"], 1)
                    if l1 and not (isinstance(p, int) and p == 0):
                        if g < 2:
                            o_stat_tiles(p - 1, g)
                        if g == 1:
                            o_mean(p - 1)
                        if g == 4:
                            o_norm(p - 1)
                    if l0 and g == 3:
                        t_rows()
                    if l0 and g >= 5:
                        att_tile(g - 5)
                    if isinstance(p, int) and p == -1:
                        if g == 7:
                            gram_top(1)
                        if g == 8:
                            gram_scales(1)
                        if g == 10:
                            u_lo(1)
                if new:
                    dve.wait_ge(s["x_loaded"], 16 * (r + 1))
                    wait(dve, s["wx_mm"], 8 * r)
                    for j in range(2):
                        dve.tensor_copy(x_hi[:, j], x_in[:, j]).then_inc(s["x_hi_done"], 1)
                if l1:
                    for k in range(4):
                        j, c = k // 2, k % 2
                        dve.wait_ge(s["s_mm"], 4 * p + j + 1)
                        block_ = halves[4 + j][:, c, c * P:(c + 1) * P]
                        last = dve.scalar_tensor_tensor(out=diag_junk[:, k, :], in0=block_, scalar=1.0, in1=ident[:],
                                                        op0=ALU.mult, op1=ALU.mult, accum_out=sq_l[:, k:k + 1])
                    last.then_inc(s["sq_l_done"], 1)
                    dve.wait_ge(s["sq_l_done"], p + 1)
                    dve.tensor_scalar(sq_lc[:], sq_l[:], c_norm[:, 0:1], None, ALU.max).then_inc(s["sq_lc_done"], 1)
                    for k in range(4):
                        j, c = k // 2, k % 2
                        dve.wait_ge(s["s_mm"], 4 * p + 3 + j)
                        block_ = halves[6 + j][:, c, c * P:(c + 1) * P]
                        last = dve.scalar_tensor_tensor(out=diag_junk[:, 4 + k, :], in0=block_, scalar=0.5,
                                                        in1=ident[:], op0=ALU.mult, op1=ALU.mult,
                                                        accum_out=sq_g[:, k:k + 1])
                    last.then_inc(s["sq_g_done"], 1)
                    dve.wait_ge(s["sq_g_done"], p + 1)
                    dve.tensor_scalar(sq_ghi[:], sq_g[:], 2.0 ** -4, None, ALU.mult).then_inc(s["sq_ghi_done"], 1)
                    dve.wait_ge(s["sq_ghi_done"], p + 1)
                    dve.scalar_tensor_tensor(out=sq_glo[:], in0=sq_g[:], scalar=2.0 ** -4, in1=sq_ghi[:],
                                             op0=ALU.mult, op1=ALU.subtract).then_inc(s["sq_glo_done"], 1)
                    for k in range(4):
                        rows = slice((k % 2) * P, (k % 2 + 1) * P)
                        dve.tensor_scalar(diag_ghi[:, k // 2, rows], ident16[:], sq_ghi[:, k:k + 1], None, ALU.mult)
                    dve.wait_ge(s["sq_glo_done"], p + 1)
                    for k in range(4):
                        rows = slice((k % 2) * P, (k % 2 + 1) * P)
                        last = dve.tensor_scalar(diag_glo[:, k // 2, rows], ident16[:], sq_glo[:, k:k + 1], None,
                                                 ALU.mult)
                        if k % 2 == 1:
                            last.then_inc(s["diag_g_done"], 1)
                    dve.wait_ge(s["r_l_done"], p + 1)
                    for k in range(4):
                        last = dve.tensor_scalar(diag_r[:, k, :], ident[:], r_l[:, k:k + 1], None, ALU.mult)
                    last.then_inc(s["diag_r_done"], 1)
                    v_lo_tile(0)
                    v_lo_tile(1)
                    for j in range(2):
                        dve.wait_ge(s["g_mm"], 2 * p + j + 1)
                        dve.wait_ge(s["diag_g_done"], 2 * p + j + 1)
                        for c in range(OC):
                            last = dve.tensor_scalar(a_g[:, j, c, :], halves[6 + j][:, c, :],
                                                     sq_g[:, 2 * j + c:2 * j + c + 1], 0.0, ALU.subtract, ALU.min)
                        last.then_inc(s["clamp_done"], 1)
                    v_lo_tile(2)
                    for j in range(2):
                        dve.wait_ge(s["r_mm"], p + 1)
                        for c in range(OC):
                            last = dve.tensor_tensor(a_l[:, j, c, :], halves[0][:, j, :], mask[:, c, :], ALU.mult)
                        last.then_inc(s["mr_done"], 1)
                    if l0:
                        den(0)
                    for k in range(4):
                        j, c = k // 2, k % 2
                        dve.wait_ge(s["mr_done"], 2 * p + j + 1)
                        last = dve.scalar_tensor_tensor(out=a_l[:, j, c, :], in0=halves[4 + j][:, c, :], scalar=0.0,
                                                        in1=a_l[:, j, c, :], op0=ALU.max, op1=ALU.mult,
                                                        accum_out=deg_l[:, k:k + 1])
                        if k == 1 and l0:
                            den(1)
                    last.then_inc(s["al_done"], 1)
                    if l0:
                        den(2)
                    for k in range(4):
                        j, c = k // 2, k % 2
                        dve.wait_ge(s["exp_done"], 2 * p + j + 1)
                        last = dve.scalar_tensor_tensor(out=a_g[:, j, c, :], in0=a_g[:, j, c, :], scalar=1.0,
                                                        in1=mask[:, c, :], op0=ALU.mult, op1=ALU.mult,
                                                        accum_out=deg_g[:, k:k + 1])
                    last.then_inc(s["ag_done"], 1)
                    if l0:
                        den(3)
                    dve.wait_ge(s["al_done"], p + 1)
                    dve.tensor_tensor(deg_l2[:], deg_l[:], r_l[:], ALU.mult).then_inc(s["dl_done"], 1)
                    dve.wait_ge(s["ag_done"], p + 1)
                    dve.tensor_scalar(deg_g2[:], deg_g[:], DEG_EPS, None, ALU.max).then_inc(s["dgr_done"], 1)
                    dve.wait_ge(s["dl_done"], 3 * p + 1)
                    dve.tensor_scalar(deg_l3[:], deg_l2[:], DEG_EPS, None, ALU.max).then_inc(s["dl_done"], 1)
                    dve.wait_ge(s["dgr_done"], 2 * p + 1)
                    dve.reciprocal(deg_g3[:], deg_g2[:]).then_inc(s["dgr_done"], 1)
                    dve.wait_ge(s["dl_done"], 3 * p + 2)
                    dve.reciprocal(deg_l4[:], deg_l3[:]).then_inc(s["dl_done"], 1)
                    dve.wait_ge(s["dgr_done"], 2 * p + 2)
                    dve.tensor_scalar(s_g[:], deg_g3[:], c_wg[:, 0:1], None, ALU.mult).then_inc(s["sg_done"], 1)
                    dve.wait_ge(s["dl_done"], 3 * p + 3)
                    dve.scalar_tensor_tensor(out=s_l[:], in0=deg_l4[:], scalar=c_wl[:, 0:1], in1=r_l[:],
                                             op0=ALU.mult, op1=ALU.mult).then_inc(s["sl_done"], 1)
                    if l0:
                        den(4)
                    dve.wait_ge(s["sl_done"], p + 1)
                    for k in range(4):
                        j, c = k // 2, k % 2
                        dve.tensor_scalar(a_l[:, j, c, :], a_l[:, j, c, :], s_l[:, k:k + 1], None, ALU.mult)\
                           .then_inc(s["kl_done"], 1)
                    dve.wait_ge(s["sg_done"], p + 1)
                    for k in range(4):
                        j, c = k // 2, k % 2
                        dve.wait_ge(s["kl_done"], 4 * p + k + 1)
                        last = dve.scalar_tensor_tensor(out=a_l[:, j, c, :], in0=a_g[:, j, c, :],
                                                        scalar=s_g[:, k:k + 1], in1=a_l[:, j, c, :],
                                                        op0=ALU.mult, op1=ALU.add)
                        if c == 1:
                            last.then_inc(s["k_done"], 1)
                            if l0:
                                den(5 + j)
                    if l0:
                        den(7)
                    for j in range(2):
                        dve.wait_ge(s["kt_hi_done"], 2 * p + j + 1)
                        dve.tensor_tensor(kt_lo[:, j], halves[4 + j], kt_hi[:, j], ALU.subtract)\
                           .then_inc(s["kt_lo_done"], 1)
                elif l0:
                    for k in range(8):
                        den(k)
                        split_wvo(k)
                    constants()
                if l0:
                    def y_stat_tile(k):
                        if k % 2:
                            dve.wait_ge(s["y_odd_done"], 2 * q + k // 2 + 1)
                        else:
                            dve.wait_ge(s["y_done"], 2 * q + k // 2 + 1)
                        dve.bn_stats(y_stat[:, k, :], y[:, k, :]).then_inc(s["y_stat_done"], 1)

                    dve.wait_ge(s["xr_loaded"], 16 * (q + 1))
                    for k in (0, 2):
                        dve.wait_ge(s["relu_done"], 4 * q + k + 1)
                        dve.tensor_tensor(y[:, k, :], y[:, k, :], x_res[:, k // 2, k % 2, :], ALU.add)\
                           .then_inc(s["y_done"], 1)
                        if k == 0:
                            y_stat_tile(0)
                    if l1:
                        v_lo_tile(3)
                    y_stat_tile(1)
                    y_stat_tile(2)
                    y_stat_tile(3)
                    wait(dve, s["y_rstd_done"], q)
                    dve.wait_ge(s["y_stat_done"], 4 * q + 4)
                    dve.tensor_scalar(turn_y[:], y_stat[:, 3, 0:1], 1.0, None, ALU.mult)
                    for k in range(4):
                        last = dve.bn_aggr(y_mv[:, k, :], y_stat[:, k, :])
                    last.then_inc(s["y_mv_done"], 1)
                elif l1:
                    v_lo_tile(3)
                if l1:
                    wait(dve, s["stored"], 32 * p)
                    for k in range(4):
                        dve.wait_ge(s["o_mm"], 4 * p + k + 1)
                        dve.scalar_tensor_tensor(out=o[:, k, :], in0=bank[late[k]][:], scalar=c_out[:, 0:1],
                                                 in1=h[:, k, :], op0=ALU.mult, op1=ALU.add).then_inc(s["o_done"], 1)
                if l0:
                    dve.wait_ge(s["y_rstd_done"], q + 1)
                    dve.wait_ge(s["y_mv_done"], q + 1)
                    wait(dve, s["o_done"], 4 * q)
                    for k in range(4):
                        dve.tensor_scalar(h[:, k, :], y[:, k, :], y_mv[:, k, 0:1], y_rstd[:, k:k + 1],
                                          ALU.subtract, ALU.mult).then_inc(s["h_done"], 1)
                if new:
                    wait(dve, s["uv_done"], r)
                    for k in range(4):
                        xw_lo_tile(k)
                if l0:
                    for d in range(DC):
                        dve.wait_ge(s["ht_hi_done"], 4 * q + d + 1)
                        dve.tensor_tensor(ht_lo[:, d, :], bank[d][:], ht_hi[:, d, :], ALU.subtract)\
                           .then_inc(s["ht_lo_done"], 1)
                if new:
                    for k in range(4, 8):
                        xw_lo_tile(k)
                if new:
                    dve.wait_ge(s["xw_lo_done"], 8 * r + 8)
                    dve.tensor_reduce(q_part[:], q_cols, AX.X, ALU.max).then_inc(s["q_part_done"], 1)
                    dve.tensor_copy(k_hi[:], qk[:, :, 1]).then_inc(s["k_hi_done"], 1)
                    dve.wait_ge(s["k_hi_done"], r + 1)
                    dve.tensor_tensor(k_lo[:], qk[:, :, 1], k_hi[:], ALU.subtract).then_inc(s["k_lo_done"], 1)
                    for n in range(2 * NC):
                        dve.tensor_scalar(dk_hi[:, n, :], ident16[:], k_hi[:, n:n + 1], None, ALU.mult)
                    dve.wait_ge(s["k_lo_done"], r + 1)
                    for n in range(2 * NC):
                        last = dve.tensor_scalar(dk_lo[:, n, :], ident16[:], k_lo[:, n:n + 1], None, ALU.mult)
                    last.then_inc(s["dk_done"], 1)
                    dve.wait_ge(s["q_max_done"], r + 1)
                    wait(dve, s["uv_done"], r)
                    for j in range(2):
                        last = dve.tensor_scalar(q_rel[:, j, :], q_cols[:, j, :], q_max[:, j:j + 1], None, ALU.subtract)
                    last.then_inc(s["q_rel_done"], 1)
                    if isinstance(p, int) and p == -2:
                        gram_top(0)
                        gram_scales(0)
                        u_lo(0)
            setup0()
            pipeline(dve, step)
            for half in range(2):
                o_stat_tiles(PAIRS - 1, half)
            o_mean(PAIRS - 1)
            o_norm(PAIRS - 1)

        @block.gpsimd
        def _(pool):
            pool.memset(ident[:], 0.0).then_inc(s["setup_p"], 1)
            pool.memset(exponent[:], -0.5).then_inc(s["setup_p"], 1)
            pool.memset(top_part[:, 5:8], 0.0).then_inc(s["setup_p"], 1)
            pool.memset(eps[:], LN_EPS).then_inc(s["setup_p"], 1)
            pool.wait_ge(s["setup_p"], 4)
            pool.affine_select(out=ident[:], in_=ident[:], compare_op=ALU.not_equal, fill=1.0, base=0,
                               pattern=[[-1, P]], channel_multiplier=1).then_inc(s["setup_p"], 1)

            def largest(cols, ready, done):
                pool.wait_ge(ready, 1)
                pool.partition_all_reduce(top_all[:, cols[0]:cols[1]], top_part[:, cols[0]:cols[1]], P, RMAX)\
                    .then_inc(done, 1)

            def cut_mask():
                pool.wait_ge(s["mask_loaded"], 16)
                pool.affine_select(out=mask[:], in_=mask[:], compare_op=ALU.not_equal, fill=0.0, base=0,
                                   pattern=[[P, OC], [-1, O]], channel_multiplier=1).then_inc(s["mask_cut"], 1)

            def step(p, l1, l0, new):
                q, r = p + 1, p + 2
                if l0:
                    wait(pool, s["ot_mm"], 8 * q)
                    for g in range(8):
                        pool.wait_ge(s["att_hi_done"], 8 * q + g + 1)
                        n = (g // NC, g % NC)
                        pool.tensor_tensor(att_lo[:, n[0], n[1], :], att[:, g % 2, :], att_hi[:, n[0], n[1], :],
                                           ALU.subtract).then_inc(s["att_lo_done"], 1)
                        if isinstance(p, int) and p == -1 and g == 1:
                            largest((3, 4), s["top_g"], s["top_g_all"])
                if l1:
                    pool.wait_ge(s["sq_lc_done"], p + 1)
                    wait(pool, s["sl_done"], p)
                    pool.tensor_tensor(r_l[:], sq_lc[:], exponent[:], ALU.pow).then_inc(s["r_l_done"], 1)
                if new:
                    if isinstance(p, int) and p == -1:
                        largest((4, 5), s["topv"], s["topv_all"])
                    wait(pool, s["wx_mm"], 8 * r)
                    for j in range(2):
                        pool.wait_ge(s["x_hi_done"], 2 * r + j + 1)
                        pool.tensor_tensor(x_lo[:, j], x_in[:, j], x_hi[:, j], ALU.subtract)\
                            .then_inc(s["x_lo_done"], 1)
                if l0:
                    pool.wait_ge(s["xr_loaded"], 16 * (q + 1))
                    for k in (1, 3):
                        pool.wait_ge(s["relu_done"], 4 * q + k + 1)
                        pool.tensor_tensor(y[:, k, :], y[:, k, :], x_res[:, k // 2, k % 2, :], ALU.add)\
                            .then_inc(s["y_odd_done"], 1)
                    pool.wait_ge(s["y_mv_done"], q + 1)
                    pool.tensor_tensor(y_var[:], y_mv[:, :, 1], eps[:], ALU.add).then_inc(s["y_var_done"], 1)
                    pool.wait_ge(s["y_var_done"], q + 1)
                    wait(pool, s["h_done"], 4 * q)
                    pool.tensor_tensor(y_rstd[:], y_var[:], exponent[:], ALU.pow).then_inc(s["y_rstd_done"], 1)
                if new:
                    pool.wait_ge(s["q_part_done"], r + 1)
                    pool.tensor_tensor(turn_q[:], q_part[:], q_part[:], ALU.add)
                    pool.partition_all_reduce(q_max[:], q_part[:], P, RMAX).then_inc(s["q_max_done"], 1)
                if isinstance(p, int) and p == -2:
                    largest((2, 3), s["top_l"], s["top_l_all"])
                    cut_mask()
                if l1:
                    pool.wait_ge(s["o_mv_done"], p + 1)
                    pool.tensor_tensor(o_var[:], o_mv[:, :, 1], eps[:], ALU.add).then_inc(s["o_var_done"], 1)
                    pool.wait_ge(s["o_var_done"], p + 1)
                    wait(pool, s["normed"], 2 * p)
                    pool.tensor_tensor(o_rstd[:], o_var[:], exponent[:], ALU.pow).then_inc(s["o_rstd_done"], 1)

            largest((0, 2), s["top0"], s["top0_all"])
            pipeline(pool, step)


_SHAPE = (32, 256, 512)


def kernel(**inputs):
    import numpy as np
    import concourse.bacc as bacc
    from concourse.bass_utils import run_bass_kernel_spmd

    a = {k: np.asarray(v) for k, v in inputs.items()}
    laid = {
        "x": a["x"],
        "adj": a["adj"],
        "adjT": a["adj"].T,
        "wqk": np.stack([a["L0_gnn_wq"], a["L0_gnn_wk"]], -1).reshape(2, P, 2).transpose(1, 0, 2),
        "bm": a["L0_gnn_bm"].reshape(2, P).T,
        "wl": a["L1_gnn_W_lang"],
        "wg": a["L1_gnn_W_grav"],
        "wv": a["L1_gnn_W_V"],
        "woT": a["L1_gnn_W_O"].T,
        "gate": np.broadcast_to(a["L1_gnn_gate_logit"].reshape(1, 1), (P, 1)),
        "sigma": np.broadcast_to(a["L1_gnn_log_sigma"].reshape(1, 1), (P, 1)),
    }
    nc = bacc.Bacc("TRN2", target_bir_lowering=False, num_devices=1)
    arrays, args = {}, []
    for name, v in laid.items():
        v = np.ascontiguousarray(v)
        arrays[f"in_{name}"] = v
        args.append(nc.dram_tensor(f"in_{name}", v.shape, mybir.dt.from_np(v.dtype), kind="ExternalInput").ap())
    args.append(nc.dram_tensor("out_y", _SHAPE, F32, kind="ExternalOutput").ap())
    build(nc, *args)
    r = run_bass_kernel_spmd(nc, [arrays], core_ids=[0])
    return r.results[0]["out_y"]
```

```python
from contextlib import ExitStack

import concourse.bass as bass
from concourse import mybir

F32 = mybir.dt.float32
F16 = mybir.dt.float16
ALU = mybir.AluOpType
ACT = mybir.ActivationFunctionType
AX = mybir.AxisListType
RMAX = bass.bass_isa.ReduceOp.max

P = 128
LN_EPS = 1e-5
DEG_EPS = 1e-8
NORM_EPS2 = 1e-16
SLOPE = 0.01
TOP = 4.0
LN256 = 5.545177444479562


def wait(engine, semaphore, count):
    if not (isinstance(count, int) and count <= 0):
        engine.wait_ge(semaphore, count)


def at(p, *steps):
    return isinstance(p, int) and p in steps


def build(nc, x, adj, adjT, wqk, bm, wl, wg, wv, woT, gate, sigma, out):
    B, C, N = x.shape
    O = adj.shape[0]
    D = wl.shape[0]
    PAIRS = B // 2
    CC, OC, NC, DC = C // P, O // P, N // P, D // P
    assert C == O == 2 * P and N == D == 4 * P

    x_v = x.rearrange("(t j) (c p) n -> t p j c n", j=2, p=P)
    out_v = out.rearrange("(t j) (c p) n -> t j p c n", j=2, p=P)

    with ExitStack() as ctx:
        def sb(name, shape, dt=F32):
            return ctx.enter_context(nc.sbuf_tensor(name, [P, *shape], dt))

        def sem(name):
            return ctx.enter_context(nc.semaphore(name))

        ident = sb("ident", [P])
        ones = sb("ones", [P])
        ident16, ones16 = sb("ident16", [P], F16), sb("ones16", [P], F16)
        ident64 = sb("ident64", [P], F16)
        mask = sb("mask", [OC, O])
        exponent = sb("exponent", [4])
        shift = sb("shift", [1])
        bias_m = sb("bias_m", [OC])
        ul_hi, ul_lo = sb("ul_hi", [DC, D], F16), sb("ul_lo", [DC, D], F16)
        ug_hi, ug_lo = sb("ug_hi", [DC, D], F16), sb("ug_lo", [DC, D], F16)
        wvo_hi, wvo_lo = sb("wvo_hi", [DC, D], F16), sb("wvo_lo", [DC, D], F16)
        OW = O + 2
        wm_hi, wm_lo = sb("wm_hi", [CC, OW], F16), sb("wm_lo", [CC, OW], F16)
        qk_raw = sb("qk_raw", [CC, 2])
        knobs = sb("knobs", [2])
        top_part, top_all = sb("top_part", [8]), sb("top_all", [8])
        scale = sb("scale", [8])
        unscale = sb("unscale", [8])
        half_scale = sb("half_scale", [2])
        top_gram = sb("top_gram", [2, 3])
        c_u, c_v, c_a, c_b = (sb(n, [1]) for n in ("c_u", "c_v", "c_a", "c_b"))
        c_grav, c_wl, c_wg, c_out = (sb(n, [1]) for n in ("c_grav", "c_wl", "c_wg", "c_out"))
        c_norm = sb("c_norm", [4])
        tiny = sb("tiny", [8])
        eps = sb("eps", [4])
        turn_q, turn_y, turn_o = sb("turn_q", [2]), sb("turn_y", [1]), sb("turn_o", [1])
        x_in = sb("x_in", [2, CC, N])
        x_res = sb("x_res", [2, CC, N])
        x_hi, x_lo = sb("x_hi", [2, CC, N], F16), sb("x_lo", [2, CC, N], F16)
        xw_hi, xw_lo = sb("xw_hi", [2, NC, OW], F16), sb("xw_lo", [2, NC, OW], F16)
        qk = sb("qk", [2 * NC, 2])
        q_part, q_max, q_rel = sb("q_part", [2]), sb("q_max", [2]), sb("q_rel", [2, NC])
        q_cols = qk[:, :, 0].rearrange("p (j n) -> p j n", j=2)
        k_hi, k_lo = sb("k_hi", [2 * NC], F16), sb("k_lo", [2 * NC])
        dk_hi, dk_lo = sb("dk_hi", [2 * NC, P], F16), sb("dk_lo", [2 * NC, P], F16)
        u_col, v_col = sb("u_col", [2, NC]), sb("v_col", [2, NC])
        a_row, b_row = sb("a_row", [2, N]), sb("b_row", [2, N])
        vb = sb("vb", [2, N])
        att = sb("att", [2, N])
        att_hi, att_lo = sb("att_hi", [2, NC, N], F16), sb("att_lo", [2, NC, N], F16)
        den_inv = sb("den_inv", [8])
        agg_t = sb("agg_t", [2, NC, O])
        y = sb("y", [2 * OC, N])
        y_stat, y_mv = sb("y_stat", [2 * OC, 6]), sb("y_mv", [2 * OC, 2])
        y_var, y_rstd = sb("y_var", [2 * OC]), sb("y_rstd", [2 * OC])
        h = sb("h", [2 * OC, N])
        ht_hi, ht_lo = sb("ht_hi", [DC, 2 * O], F16), sb("ht_lo", [DC, 2 * O], F16)
        z_hi, z_lo = sb("z_hi", [2 * DC, 2 * O], F16), sb("z_lo", [2 * DC, 2 * O], F16)
        t_hi, t_lo = sb("t_hi", [4, OC, O], F16), sb("t_lo", [4, OC, O], F16)
        v_hi, v_lo = sb("v_hi", [2 * OC, D], F16), sb("v_lo", [2 * OC, D], F16)
        diag_junk = sb("diag_junk", [8, P])
        sq_l, sq_lc, r_l = sb("sq_l", [4]), sb("sq_lc", [4]), sb("r_l", [4])
        neg_g = sb("neg_g", [4])
        diag_r = sb("diag_r", [4, P])
        a_l, a_g = sb("a_l", [2, OC, O]), sb("a_g", [2, OC, O])
        deg_l, deg_l2, deg_l3, deg_l4, s_l = (sb(n, [4]) for n in ("deg_l", "deg_l2", "deg_l3", "deg_l4", "s_l"))
        deg_g, deg_g2, deg_g3, s_g = (sb(n, [4]) for n in ("deg_g", "deg_g2", "deg_g3", "s_g"))
        kt_hi, kt_lo = sb("kt_hi", [2, OC, O], F16), sb("kt_lo", [2, OC, O], F16)
        o = sb("o", [2 * OC, N])
        o_stat, o_mv = sb("o_stat", [2 * OC, 6]), sb("o_mv", [2 * OC, 2])
        o_var, o_rstd = sb("o_var", [2 * OC]), sb("o_rstd", [2 * OC])
        wl_raw = agg_t[:].rearrange("p j c n -> p (j c n)").rearrange("p (c n) -> p c n", c=DC)
        wg_raw, wv_raw, wo_raw = y[:], o[:], h[:]
        adjT_raw = att[:].rearrange("p a n -> p (a n)")[:, 0:CC * O].rearrange("p (c n) -> p c n", c=CC)

        bank = [ctx.enter_context(nc.psum_tensor(f"bank{i}", [P, 512], F32)) for i in range(8)]
        halves = [b[:].rearrange("p (c n) -> p c n", c=2) for b in bank]

        wvo_bank = (7, 4, 5, 3)
        gram_rows = (((0, 3, 0), (1, 1, 0), (3, 1, 3 * P), (2, 2, 0)),
                     ((0, 0, 0), (1, 6, 0), (3, 6, 3 * P), (2, 2, 2 * P)))
        v_bank = (0, 1, 2, 7)
        late = (6, 5, 7, 4)
        T_HI_AT, T_LO_AT = (8, 10, 12), (9, 11)
        names = """x_loaded xr_loaded small_loaded wl0_loaded wl1_loaded wl2_loaded wl3_loaded wg_loaded
            wv_loaded wo_loaded mask_loaded stored consts_set mask_cut top0 top0_all top_l top_l_all
            top_g top_g_all topv topv_all scales0 scales_l scales_g scalev half_l half_g gram_mm
            gram_part u_hi_done u_lo_done unscale_done coef_done pool_set wm_hi_done wqk_hi_done
            wvo_hi_done wm_lo_done wqk_lo_done wvo_lo_done wvo_mm knobs_done tiny_done x_hi_done
            x_lo_done wx_mm xw_hi_done xw_lo_done k_mm k_hi_done k_lo_done dk_hi_done dk_lo_done
            q_part_done q_max_done q_rel_done uv_done t_done ab_done vb_done att_done att_hi_done
            att_lo_done ot_mm den_done agg_done to_mm relu_done y_done y_odd_done y_stat_done y_mv_done
            y_var_done y_rstd_done h_done ht_mm ht_hi_done ht_lo_done z_mm z_hi_done z_lo_done t_mm
            t_hi_done t_lo_done s_mm sq_l_done sq_lc_done r_l_done neg_g_done shift_done diag_r_done
            clamp_done exp_done v_mm v_hi_done v_lo_done r_mm mr_done al_done dl_done sl_done ag_done
            dgr_done sg_done kl_done k_done kt_mm kt_hi_done kt_lo_done o_mm o_done o_stat_done
            o_mv_done o_var_done o_rstd_done normed""".split()
        s = {n: sem(n) for n in names}

        block = ctx.enter_context(nc.Block())

        def pipeline(engine, step):
            step(-2, False, False, True)
            step(-1, False, True, True)
            step(0, True, True, True)
            with engine.Fori(1, PAIRS - 2) as p:
                step(p, True, True, True)
            step(PAIRS - 2, True, True, False)
            step(PAIRS - 1, True, False, False)

        @block.sync
        def _(sp):
            for f in range(DC):
                sp.dma_start(wl_raw[:, f, :], wl[f * P:(f + 1) * P, :]).then_inc(s[f"wl{f}_loaded"], 16)
            sp.dma_start(adjT_raw, adjT.rearrange("(c p) o -> p c o", p=P)).then_inc(s["small_loaded"], 16)
            sp.dma_start(qk_raw[:], wqk).then_inc(s["small_loaded"], 16)
            sp.dma_start(bias_m[:], bm).then_inc(s["small_loaded"], 16)
            sp.dma_start(knobs[:, 0:1], gate).then_inc(s["small_loaded"], 16)
            sp.dma_start(knobs[:, 1:2], sigma).then_inc(s["small_loaded"], 16)

            def step(p, l1, l0, new):
                q, r = p + 1, p + 2
                if l0:
                    wait(sp, s["y_done"], 2 * q)
                    wait(sp, s["y_odd_done"], 2 * q)
                    wait(sp, s["x_loaded"], 16 * (q + 1))
                    sp.dma_start(x_res[:], x_in[:]).then_inc(s["xr_loaded"], 16)
                if new:
                    wait(sp, s["x_lo_done"], 2 * r)
                    wait(sp, s["xr_loaded"], 16 * r)
                    sp.dma_start(x_in[:], x_v[r]).then_inc(s["x_loaded"], 16)
                if at(p, -2):
                    sp.dma_start(wg_raw, wg.rearrange("(c p) d -> p c d", p=P)).then_inc(s["wg_loaded"], 16)
                    sp.dma_start(wv_raw, wv.rearrange("(c p) d -> p c d", p=P)).then_inc(s["wv_loaded"], 16)
                    sp.dma_start(wo_raw, woT.rearrange("(c p) e -> p c e", p=P)).then_inc(s["wo_loaded"], 16)
                    sp.dma_start(mask[:], adj.rearrange("(c p) m -> p c m", p=P)).then_inc(s["mask_loaded"], 16)
                if l1:
                    for j in range(2):
                        sp.wait_ge(s["normed"], 2 * p + j + 1)
                        sp.dma_start(out_v[p, j], o[:, 2 * j:2 * j + 2, :]).then_inc(s["stored"], 16)

            pipeline(sp, step)
            sp.wait_ge(s["stored"], 32 * PAIRS)

        @block.tensor
        def _(pe):
            def product(dst, parts, skip=False, first=True):
                n = len(parts)
                for i, (ah, al, bh, bl) in enumerate(parts):
                    pe.matmul(dst, ah, bh, start=(i == 0 and first), stop=False, skip_group_check=skip)
                    pe.matmul(dst, ah, bl, start=False, stop=False, skip_group_check=skip)
                    last = pe.matmul(dst, al, bh, start=False, stop=(i == n - 1), skip_group_check=skip)
                return last

            def gram(kind, between):
                raw = (wl_raw, wg_raw)[kind]
                if kind == 1:
                    pe.wait_ge(s["wg_loaded"], 16)
                for i, (d, b, col) in enumerate(gram_rows[kind]):
                    width = D - d * P
                    if i == 2 + kind:
                        between()
                    if kind == 1 and i == 1:
                        pe.wait_ge(s["xw_lo_done"], 8)
                    if kind == 1 and i == 3:
                        pe.wait_ge(s["u_lo_done"], 1)
                    for f in range(DC):
                        if kind == 0 and i == 0:
                            pe.wait_ge(s[f"wl{f}_loaded"], 16)
                        last = pe.matmul(bank[b][:, col:col + width], raw[:, f, d * P:(d + 1) * P],
                                         raw[:, f, d * P:D], start=(f == 0 and i != 2),
                                         stop=(f == DC - 1), skip_group_check=True)
                last.then_inc(s["gram_mm"], 1)

            def fuse_weights(rows):
                pe.wait_ge(s["wv_loaded"], 16)
                pe.wait_ge(s["wo_loaded"], 16)
                pe.wait_ge(s["t_done"], 2)
                for d in rows:
                    if d == DC - 1:
                        pe.wait_ge(s["u_lo_done"], 1)
                    for f in range(DC):
                        last = pe.matmul(bank[wvo_bank[d]][:], wv_raw[:, f, d * P:(d + 1) * P], wo_raw[:, f, :],
                                         start=(f == 0), stop=(f == DC - 1))
                    last.then_inc(s["wvo_mm"], 1)

            def step(p, l1, l0, new):
                q, r = p + 1, p + 2
                x_first = at(p, -1)

                def k_rows():
                    pe.wait_ge(s["dk_hi_done"], q + 1)
                    pe.wait_ge(s["dk_lo_done"], q + 1)
                    for j, b in ((0, 7), (1, 4)):
                        pe.wait_ge(s["xw_lo_done"], 8 * q + 8)
                        n = slice(j * NC, (j + 1) * NC)
                        pe.matmul(bank[b][:], ones16[:], dk_hi[:, n, :].rearrange("p a n -> p (a n)"),
                                  start=True, stop=False)
                        pe.matmul(bank[b][:], ones16[:], dk_lo[:, n, :].rearrange("p a n -> p (a n)"),
                                  start=False, stop=True).then_inc(s["k_mm"], 1)

                if l0 and not l1:
                    k_rows()
                    gram(1, between=lambda: fuse_weights((0,)))
                    fuse_weights((1, 2, 3))
                if l1:
                    up = at(p, 0, PAIRS - 1)
                    e_order = range(DC) if up else range(DC - 1, -1, -1)
                    for g in range(8):
                        hi, lo = (ul_hi, ul_lo) if g < 4 else (ug_hi, ug_lo)
                        block_e = e_order[g % 4]
                        e = slice(block_e * P, (block_e + 1) * P)
                        if g == 0 and not up:
                            pe.wait_ge(s["ht_lo_done"], 4 * p + 4)
                        if g < 4 and up:
                            pe.wait_ge(s["ht_lo_done"], 4 * p + g + 1)
                        if g >= 4:
                            pe.wait_ge(s["z_lo_done"], 8 * p + g - 3)
                        product(bank[g % 4][:], [(hi[:, d, e], lo[:, d, e], ht_hi[:, d, :], ht_lo[:, d, :])
                                                 for d in range(block_e + 1)]).then_inc(s["z_mm"], 1)
                        if l0 and g == (3 if up else 1):
                            k_rows()

                    def t_product(k):
                        kind, j = k // 2, k % 2
                        pe.wait_ge(s["z_lo_done"], 8 * p + 4 * kind + 4)
                        if k == 0:
                            if l0:
                                pe.wait_ge(s["t_done"], 2 * q + 2)
                                pe.wait_ge(s["xw_lo_done"], 8 * q + 8)
                            else:
                                pe.wait_ge(s["o_done"], 4 * p)
                        cols = slice(j * O, (j + 1) * O)
                        for c in range(OC):
                            rows = slice(j * O + c * P, j * O + (c + 1) * P)
                            last = product(halves[4 + k][:, c, :],
                                           [(z_hi[:, 4 * kind + g, rows], z_lo[:, 4 * kind + g, rows],
                                             ht_hi[:, e_order[g], cols], ht_lo[:, e_order[g], cols])
                                            for g in range(DC)], skip=True, first=(c == 0))
                        last.then_inc(s["t_mm"], 1)

                    def add_transposed(k):
                        pe.wait_ge(s["t_lo_done"], 4 * p + k + 1)
                        for c in range(OC):
                            for m in range(OC):
                                for part in (t_hi, t_lo):
                                    last = pe.matmul(halves[4 + k][:, c, m * P:(m + 1) * P],
                                                     part[:, k, m, c * P:(c + 1) * P], ident64[:],
                                                     start=False, stop=True, skip_group_check=True)
                        last.then_inc(s["s_mm"], 1)

                    t_product(0)
                    t_product(1)
                    t_product(2)
                    t_product(3)

                    if at(p, 0):
                        pe.wait_ge(s["wvo_lo_done"], 4)

                    def v_product(k):
                        rows = slice(k * P, (k + 1) * P)
                        pe_last = product(bank[v_bank[k]][:], [(ht_hi[:, d, rows], ht_lo[:, d, rows],
                                                        wvo_hi[:, d, :], wvo_lo[:, d, :]) for d in range(DC)])
                        pe_last.then_inc(s["v_mm"], 1)

                    def norm_rows():
                        pe.wait_ge(s["diag_r_done"], p + 1)
                        pe.matmul(bank[3][:], ones[:], diag_r[:].rearrange("p a n -> p (a n)"),
                                  start=True, stop=True).then_inc(s["r_mm"], 1)

                    v_product(0)
                    add_transposed(0)
                    add_transposed(1)
                    if l0:
                        v_product(1)
                    add_transposed(2)
                    add_transposed(3)
                    if l0:
                        v_product(2)
                    else:
                        norm_rows()
                        v_product(1)
                        v_product(2)

                if l0:
                    for k in range(8):
                        j, m = k // NC, slice((k % NC) * P, (k % NC + 1) * P)
                        pe.wait_ge(s["att_lo_done"], 8 * q + 4 * j + 4)
                        if k == 0:
                            pe.wait_ge(s["xw_lo_done"], 8 * q + 8)
                            if at(p, -1):
                                pe.wait_ge(s["u_lo_done"], 2)
                        if l1 and k < 3:
                            pe.wait_ge(s["v_lo_done"], 4 * p + k + 1)
                        if l1 and k == 3:
                            pe.wait_ge(s["mr_done"], 2 * p + 2)
                        if at(p, -1) and k == 3:
                            pe.wait_ge(s["wvo_lo_done"], 1)
                        if k >= 4:
                            pe.wait_ge(s["agg_done"], 8 * q + k - 3)
                        product(bank[k % 4][:, 0:O + 1], [(att_hi[:, j, n, m], att_lo[:, j, n, m],
                                                           xw_hi[:, j, n, 0:O + 1], xw_lo[:, j, n, 0:O + 1])
                                                          for n in range(NC)]).then_inc(s["ot_mm"], 1)
                        if l1 and k == 0:
                            norm_rows()

                def last_v():
                    pe.wait_ge(s["clamp_done"], 2 * p + 2)
                    v_product(3)

                if l1 and not l0:
                    last_v()
                if l1:
                    for j in range(2):
                        pe.wait_ge(s["k_done"], 2 * p + j + 1)
                        for c in range(OC):
                            for m in range(OC):
                                last = pe.transpose(halves[4 + j][:, m, c * P:(c + 1) * P],
                                                    a_l[:, j, c, m * P:(m + 1) * P], ident[:])
                        last.then_inc(s["kt_mm"], 1)
                if l0:
                    pe.wait_ge(s["agg_done"], 8 * q + 8)
                    for k in range(4):
                        j, c = k // 2, slice((k % 2) * P, (k % 2 + 1) * P)
                        for m in range(NC):
                            last = pe.transpose(bank[k][:, m * P:(m + 1) * P], agg_t[:, j, m, c], ident[:])
                        last.then_inc(s["to_mm"], 1)
                if l1 and l0:
                    last_v()
                if l1:
                    for k in range(4):
                        j, c = k // 2, slice((k % 2) * P, (k % 2 + 1) * P)
                        if k == 0:
                            pe.wait_ge(s["kt_lo_done"], 2 * p + 1)
                            pe.wait_ge(s["v_lo_done"], 4 * p + 2)
                        if k == 1:
                            pe.wait_ge(s["kt_lo_done"], 2 * p + 2)
                        if k == 2:
                            pe.wait_ge(s["v_lo_done"], 4 * p + 4)
                        product(bank[late[k]][:], [(kt_hi[:, j, m, c], kt_lo[:, j, m, c],
                                                      v_hi[:, 2 * j + m, :], v_lo[:, 2 * j + m, :])
                                                     for m in range(OC)]).then_inc(s["o_mm"], 1)

                def wx_product(k):
                    j, n = k // NC, slice((k % NC) * P, (k % NC + 1) * P)
                    if at(p, -1) and k < 4:
                        pe.wait_ge(s["wvo_lo_done"], 4)
                    if k % 4 == 0:
                        pe.wait_ge(s["x_lo_done"], 2 * r + j + 1)
                    if k < 4:
                        wait(pe, s["o_done"], 4 * p + k + 1)
                    else:
                        pe.wait_ge(s["xw_lo_done"], 8 * r + k - 3)
                    product(bank[late[k % 4]][:, 0:OW],
                            [(x_hi[:, j, c, n], x_lo[:, j, c, n], wm_hi[:, c, :], wm_lo[:, c, :])
                             for c in range(CC)]).then_inc(s["wx_mm"], 1)

                def wx_first():
                    pe.wait_ge(s["wm_lo_done"], 1)
                    pe.wait_ge(s["wqk_lo_done"], 1)
                    for k in range(8):
                        wx_product(k)

                if at(p, -2):
                    gram(0, between=wx_first)
                elif new:
                    for k in range(8 if x_first else 4):
                        wx_product(k)
                if l0:
                    pe.wait_ge(s["h_done"], 4 * q + 4)
                    for d in range(DC):
                        for k in range(4):
                            last = pe.transpose(bank[d][:, k * P:(k + 1) * P], h[:, k, d * P:(d + 1) * P], ident[:])
                        last.then_inc(s["ht_mm"], 1)
                if new and not at(p, -2, -1):
                    for k in range(4, 8):
                        wx_product(k)

            pe.wait_ge(s["consts_set"], 7)
            pe.wait_ge(s["pool_set"], 5)
            pipeline(pe, step)

        @block.scalar
        def _(act):
            def split_setup0():
                act.wait_ge(s["scales0"], 1)
                act.activation(wm_hi[:, :, 0:O], adjT_raw, ACT.Copy, scale=scale[:, 0:1]).then_inc(s["wm_hi_done"], 1)
                act.activation(wm_hi[:, :, O:OW], qk_raw[:], ACT.Copy, scale=scale[:, 1:2]).then_inc(s["wqk_hi_done"], 1)
                act.activation(tiny[:, 0:1], knobs[:, 0:1], ACT.Exp, scale=-1.0)
                act.activation(tiny[:, 1:2], knobs[:, 1:2], ACT.Exp, scale=-2.0).then_inc(s["knobs_done"], 1)

            def u_hi(kind):
                act.wait_ge(s[("half_l", "half_g")[kind]], 1)
                hi = (ul_hi, ug_hi)[kind]
                for d, b, col in gram_rows[kind]:
                    last = act.activation(hi[:, d, d * P:(d + 1) * P], bank[b][:, col:col + P], ACT.Copy,
                                          scale=half_scale[:, kind:kind + 1])
                    if d < DC - 1:
                        last = act.activation(hi[:, d, (d + 1) * P:D], bank[b][:, col + P:col + D - d * P], ACT.Copy,
                                              scale=scale[:, 2 + kind:3 + kind])
                last.then_inc(s["u_hi_done"], 1)

            def wvo_hi_tile(d):
                act.wait_ge(s["scalev"], 1)
                act.activation(wvo_hi[:, d, :], bank[wvo_bank[d]][:], ACT.Copy, scale=scale[:, 4:5])\
                   .then_inc(s["wvo_hi_done"], 1)

            def step(p, l1, l0, new):
                q, r = p + 1, p + 2

                def vb_tile(g):
                    j, n = g // NC, g % NC
                    act.wait_ge(s["ab_done"], 2 * q + j + 1)
                    act.wait_ge(s["uv_done"], q + 1)
                    wait(act, s["att_done"], 8 * q + g - 1)
                    act.activation(vb[:, g % 2, :], b_row[:, j, :], ACT.Copy, scale=v_col[:, j, n:n + 1])\
                       .then_inc(s["vb_done"], 1)

                def att_hi_tile(g):
                    wait(act, s["ot_mm"], 8 * q)
                    act.wait_ge(s["att_done"], 8 * q + g + 1)
                    act.activation(att_hi[:, g // NC, g % NC, :], att[:, g % 2, :], ACT.Copy)\
                       .then_inc(s["att_hi_done"], 1)

                def ab_rows():
                    for j in range(2):
                        act.wait_ge(s["t_done"], 2 * q + j + 1)
                        act.activation(a_row[:, j, :], a_row[:, j, :], ACT.Exp, bias=shift[:, 0:1], scale=c_a[:, 0:1])
                        act.activation(b_row[:, j, :], b_row[:, j, :], ACT.Exp, bias=shift[:, 0:1], scale=c_b[:, 0:1])\
                           .then_inc(s["ab_done"], 1)

                def t_hi_tile(k):
                    act.wait_ge(s["t_mm"], 4 * p + k + 1)
                    if k < 2:
                        source = halves[4 + k]
                    else:
                        j = k - 2
                        act.wait_ge(s["neg_g_done"], 2 * p + j + 1)
                        for c in range(OC):
                            last = act.activation(a_g[:, j, c, :], halves[4 + k][:, c, :], ACT.Identity,
                                                  bias=neg_g[:, 2 * j + c:2 * j + c + 1])
                        last.then_inc(s["shift_done"], 1)
                        act.wait_ge(s["shift_done"], 2 * p + j + 1)
                        source = a_g[:, j]
                    act.activation(t_hi[:, k], source, ACT.Copy, scale=2.0 ** -6).then_inc(s["t_hi_done"], 1)

                def v_hi_tile(k):
                    act.wait_ge(s["v_mm"], 4 * p + k + 1)
                    act.activation(v_hi[:, k, :], bank[v_bank[k]][:], ACT.Copy).then_inc(s["v_hi_done"], 1)

                for g in range(8 + 6):
                    if l1 and g < 8:
                        act.wait_ge(s["z_mm"], 8 * p + g + 1)
                        act.activation(z_hi[:, g, :], bank[g % 4][:], ACT.Copy).then_inc(s["z_hi_done"], 1)
                    if l0 and g == 4:
                        ab_rows()
                    if l0 and 5 <= g < 13:
                        vb_tile(g - 5)
                    if l0 and g >= 6:
                        att_hi_tile(g - 6)
                    if l1 and g in T_HI_AT:
                        t_hi_tile(T_HI_AT.index(g))
                    if at(p, -1):
                        if g == 6:
                            u_hi(0)
                        if g == 12:
                            u_hi(1)
                if l1:
                    t_hi_tile(3)
                    for k in range(3 if l0 else 1):
                        v_hi_tile(k)
                    for j in range(2):
                        act.wait_ge(s["clamp_done"], 2 * p + j + 1)
                        act.activation(a_g[:, j], a_g[:, j], ACT.Exp, scale=c_grav[:, 0:1]).then_inc(s["exp_done"], 1)
                if at(p, -1):
                    for d in (3, 0, 1, 2):
                        wvo_hi_tile(d)
                elif new and l1:
                    act.wait_ge(s["x_loaded"], 16 * (r + 1))
                    act.wait_ge(s["wx_mm"], 8 * r)
                    for j in range(2):
                        act.activation(x_hi[:, j], x_in[:, j], ACT.Copy).then_inc(s["x_hi_done"], 1)
                if l0:
                    for k in range(8):
                        act.wait_ge(s["den_done"], 8 * q + k + 1)
                        act.activation(agg_t[:, k // NC, k % NC, :], bank[k % 4][:, 0:O], ACT.Copy,
                                       scale=den_inv[:, k:k + 1]).then_inc(s["agg_done"], 1)
                if l1 and not l0:
                    v_hi_tile(1)
                    v_hi_tile(2)
                    v_hi_tile(3)
                if l1:
                    for j in range(2):
                        act.wait_ge(s["kt_mm"], 2 * p + j + 1)
                        act.activation(kt_hi[:, j], halves[4 + j], ACT.Copy).then_inc(s["kt_hi_done"], 1)
                if l0:
                    wait(act, s["h_done"], 4 * q)
                    for k in range(4):
                        act.wait_ge(s["to_mm"], 4 * q + k + 1)
                        act.activation(y[:, k, :], bank[k][:], ACT.Relu, bias=bias_m[:, k % 2:k % 2 + 1],
                                       scale=unscale[:, 0:1]).then_inc(s["relu_done"], 1)
                if l1 and l0:
                    v_hi_tile(3)

                def xw_hi_tile(k):
                    act.wait_ge(s["wx_mm"], 8 * r + k + 1)
                    act.activation(xw_hi[:, k // NC, k % NC, 0:O], bank[late[k % 4]][:, 0:O], ACT.Copy)\
                       .then_inc(s["xw_hi_done"], 1)

                if new:
                    for k in range(8 if at(p, -1) else 4):
                        xw_hi_tile(k)
                if l0:
                    for d in range(DC):
                        act.wait_ge(s["ht_mm"], 4 * q + d + 1)
                        act.activation(ht_hi[:, d, :], bank[d][:], ACT.Copy).then_inc(s["ht_hi_done"], 1)
                if new and not at(p, -1):
                    for k in range(4, 8):
                        xw_hi_tile(k)
                if new:
                    act.wait_ge(s["k_lo_done"], r + 1)
                    wait(act, s["k_mm"], 2 * r)
                    for n in range(2 * NC):
                        last = act.activation(dk_lo[:, n, :], ident16[:], ACT.Copy, scale=k_lo[:, n:n + 1])
                    last.then_inc(s["dk_lo_done"], 1)
                    act.wait_ge(s["q_rel_done"], r + 1)
                    wait(act, s["att_done"], 8 * r)
                    wait(act, s["vb_done"], 8 * r)
                    act.activation(u_col[:], q_rel[:], ACT.Exp, scale=c_u[:, 0:1])
                    act.activation(v_col[:], q_rel[:], ACT.Exp, scale=c_v[:, 0:1]).then_inc(s["uv_done"], 1)

            split_setup0()
            act.wait_ge(s["coef_done"], 1)
            act.wait_ge(s["consts_set"], 7)
            pipeline(act, step)

        @block.vector
        def _(dve):
            def scales(cols, ready, done, count):
                lo, hi = cols
                dve.wait_ge(ready, 1)
                dve.tensor_scalar(unscale[:, lo:hi], top_all[:, lo:hi], 1e-30, 1.0 / TOP, ALU.max, ALU.mult)\
                   .then_inc(s["unscale_done"], 1)
                dve.wait_ge(s["unscale_done"], count)
                dve.reciprocal(scale[:, lo:hi], unscale[:, lo:hi]).then_inc(done, 1)

            def setup0():
                dve.memset(ones[:], 1.0).then_inc(s["consts_set"], 1)
                dve.memset(ones16[:], 1.0).then_inc(s["consts_set"], 1)
                dve.wait_ge(s["pool_set"], 5)
                dve.tensor_copy(ident16[:], ident[:]).then_inc(s["consts_set"], 1)
                dve.tensor_scalar(ident64[:], ident[:], 64.0, None, ALU.mult).then_inc(s["consts_set"], 1)
                dve.memset(xw_hi[:, :, :, O:OW], 1.0).then_inc(s["consts_set"], 1)
                dve.memset(xw_lo[:, :, :, O:OW], 0.0).then_inc(s["consts_set"], 1)
                dve.memset(shift[:], LN256).then_inc(s["consts_set"], 1)
                dve.wait_ge(s["small_loaded"], 80)
                dve.tensor_reduce(top_part[:, 0:1], adjT_raw, AX.XY, ALU.max, apply_absolute_value=True)
                dve.tensor_reduce(top_part[:, 1:2], qk_raw[:], AX.XY, ALU.max, apply_absolute_value=True)\
                   .then_inc(s["top0"], 1)
                dve.wait_ge(s["consts_set"], 7)
                scales((0, 2), s["top0_all"], s["scales0"], 1)
                dve.wait_ge(s["wm_hi_done"], 1)
                dve.wait_ge(s["scales0"], 1)
                dve.scalar_tensor_tensor(out=wm_lo[:, :, 0:O], in0=adjT_raw, scalar=scale[:, 0:1], in1=wm_hi[:, :, 0:O],
                                         op0=ALU.mult, op1=ALU.subtract).then_inc(s["wm_lo_done"], 1)
                dve.wait_ge(s["wqk_hi_done"], 1)
                dve.scalar_tensor_tensor(out=wm_lo[:, :, O:OW], in0=qk_raw[:], scalar=scale[:, 1:2], in1=wm_hi[:, :, O:OW],
                                         op0=ALU.mult, op1=ALU.subtract).then_inc(s["wqk_lo_done"], 1)
                dve.tensor_scalar(c_u[:], unscale[:, 1:2], 1.0, None, ALU.mult)
                dve.tensor_scalar(c_v[:], unscale[:, 1:2], SLOPE, None, ALU.mult)
                dve.tensor_scalar(c_a[:], unscale[:, 1:2], 1.0 - SLOPE, None, ALU.mult)
                dve.tensor_scalar(c_b[:], unscale[:, 1:2], SLOPE - 1.0, None, ALU.mult).then_inc(s["coef_done"], 1)

            def gram_top(kind):
                dve.wait_ge(s["gram_mm"], kind + 1)
                for i, (b, lo, hi) in enumerate((((3, 0, D), (1, 0, D), (2, 0, 2 * P)),
                                                 ((0, 0, D), (6, 0, D), (2, 2 * P, D)))[kind]):
                    last = dve.tensor_reduce(top_gram[:, kind, i:i + 1], bank[b][:, lo:hi], AX.X, ALU.max,
                                             apply_absolute_value=True)
                last.then_inc(s["gram_part"], 1)
                dve.wait_ge(s["gram_part"], kind + 1)
                dve.tensor_reduce(top_part[:, 2 + kind:3 + kind], top_gram[:, kind, :], AX.X, ALU.max)\
                   .then_inc(s[("top_l", "top_g")[kind]], 1)

            def gram_scales(kind):
                ready, done, half = (("top_l_all", "scales_l", "half_l"), ("top_g_all", "scales_g", "half_g"))[kind]
                scales((2 + kind, 3 + kind), s[ready], s[done], 2 + kind)
                dve.wait_ge(s[done], 1)
                dve.tensor_scalar(half_scale[:, kind:kind + 1], scale[:, 2 + kind:3 + kind], 0.5, None, ALU.mult)\
                   .then_inc(s[half], 1)

            def u_lo(kind):
                dve.wait_ge(s["u_hi_done"], kind + 1)
                dve.wait_ge(s[("half_l", "half_g")[kind]], 1)
                hi, lo = ((ul_hi, ul_lo), (ug_hi, ug_lo))[kind]
                for d, b, col in gram_rows[kind]:
                    own, rest = slice(d * P, (d + 1) * P), slice((d + 1) * P, D)
                    last = dve.scalar_tensor_tensor(out=lo[:, d, own], in0=bank[b][:, col:col + P],
                                                    scalar=half_scale[:, kind:kind + 1], in1=hi[:, d, own],
                                                    op0=ALU.mult, op1=ALU.subtract)
                    if d < DC - 1:
                        last = dve.scalar_tensor_tensor(out=lo[:, d, rest], in0=bank[b][:, col + P:col + D - d * P],
                                                        scalar=scale[:, 2 + kind:3 + kind], in1=hi[:, d, rest],
                                                        op0=ALU.mult, op1=ALU.subtract)
                last.then_inc(s["u_lo_done"], 1)

            def wvo_top(rows):
                for d in rows:
                    dve.wait_ge(s["wvo_mm"], d + 1)
                    dve.tensor_reduce(tiny[:, 2 + d:3 + d], bank[wvo_bank[d]][:], AX.X, ALU.max,
                                      apply_absolute_value=True).then_inc(s["tiny_done"], 1)
                if d < DC - 1:
                    return
                dve.wait_ge(s["tiny_done"], DC)
                dve.tensor_reduce(top_part[:, 4:5], tiny[:, 2:2 + DC], AX.X, ALU.max).then_inc(s["topv"], 1)

            def wvo_lo_tiles():
                for i, d in enumerate((3, 0, 1, 2)):
                    dve.wait_ge(s["wvo_hi_done"], i + 1)
                    dve.scalar_tensor_tensor(out=wvo_lo[:, d, :], in0=bank[wvo_bank[d]][:], scalar=scale[:, 4:5],
                                             in1=wvo_hi[:, d, :], op0=ALU.mult, op1=ALU.subtract)\
                       .then_inc(s["wvo_lo_done"], 1)

            def constants():
                dve.wait_ge(s["knobs_done"], 1)
                dve.tensor_scalar(tiny[:, 6:7], tiny[:, 0:1], 1.0, None, ALU.add).then_inc(s["tiny_done"], 1)
                dve.wait_ge(s["tiny_done"], 5)
                dve.reciprocal(tiny[:, 7:8], tiny[:, 6:7]).then_inc(s["tiny_done"], 1)
                dve.wait_ge(s["tiny_done"], 6)
                dve.tensor_scalar(c_wl[:], tiny[:, 7:8], 256.0, None, ALU.mult)
                dve.tensor_scalar(c_wg[:], tiny[:, 7:8], -256.0, 256.0, ALU.mult, ALU.add)
                dve.tensor_scalar(c_out[:], unscale[:, 4:5], 1.0 / 256.0, None, ALU.mult)
                dve.tensor_scalar(c_grav[:], tiny[:, 1:2], unscale[:, 3:4], None, ALU.mult)
                dve.tensor_scalar(tiny[:, 6:7], scale[:, 2:3], NORM_EPS2, None, ALU.mult).then_inc(s["coef_done"], 1)
                dve.wait_ge(s["coef_done"], 2)
                dve.tensor_scalar(c_norm[:], ones[:, 0:4], tiny[:, 6:7], None, ALU.mult).then_inc(s["coef_done"], 1)
                dve.wait_ge(s["coef_done"], 3)
                dve.wait_ge(s["mask_cut"], 1)

            def o_stat_tile(pair, k):
                dve.wait_ge(s["o_done"], 4 * pair + k + 1)
                dve.bn_stats(o_stat[:, k, :], o[:, k, :]).then_inc(s["o_stat_done"], 1)

            def o_mean(pair):
                dve.wait_ge(s["o_stat_done"], 4 * pair + 4)
                dve.tensor_scalar(turn_o[:], o_stat[:, 3, 0:1], 1.0, None, ALU.mult)
                for k in range(4):
                    last = dve.bn_aggr(o_mv[:, k, :], o_stat[:, k, :])
                last.then_inc(s["o_mv_done"], 1)

            def o_norm(pair):
                dve.wait_ge(s["o_rstd_done"], pair + 1)
                dve.wait_ge(s["o_mv_done"], pair + 1)
                for k in range(4):
                    last = dve.tensor_scalar(o[:, k, :], o[:, k, :], o_mv[:, k, 0:1], o_rstd[:, k:k + 1],
                                             ALU.subtract, ALU.mult)
                    if k % 2 == 1:
                        last.then_inc(s["normed"], 1)

            def step(p, l1, l0, new):
                q, r = p + 1, p + 2
                x_first = at(p, -1)

                def den(k):
                    dve.wait_ge(s["ot_mm"], 8 * q + k + 1)
                    wait(dve, s["agg_done"], 8 * p + k + 1)
                    dve.reciprocal(den_inv[:, k:k + 1], bank[k % 4][:, O:O + 1])\
                       .then_inc(s["den_done"], 1)

                def v_lo_tile(k):
                    dve.wait_ge(s["v_hi_done"], 4 * p + k + 1)
                    dve.tensor_tensor(v_lo[:, k, :], bank[v_bank[k]][:], v_hi[:, k, :], ALU.subtract)\
                       .then_inc(s["v_lo_done"], 1)

                def xw_lo_tile(k):
                    dve.wait_ge(s["xw_hi_done"], 8 * r + k + 1)
                    dve.tensor_copy(qk[:, k, :], bank[late[k % 4]][:, O:OW])
                    dve.tensor_tensor(xw_lo[:, k // NC, k % NC, 0:O], bank[late[k % 4]][:, 0:O],
                                      xw_hi[:, k // NC, k % NC, 0:O], ALU.subtract).then_inc(s["xw_lo_done"], 1)

                def t_lo_tile(k):
                    dve.wait_ge(s["t_hi_done"], 4 * p + k + 1)
                    if k < 2:
                        for c in range(OC):
                            last = dve.scalar_tensor_tensor(out=diag_junk[:, 2 * k + c, :],
                                                            in0=halves[4 + k][:, c, c * P:(c + 1) * P], scalar=2.0,
                                                            in1=ident[:], op0=ALU.mult, op1=ALU.mult,
                                                            accum_out=sq_l[:, 2 * k + c:2 * k + c + 1])
                        last.then_inc(s["sq_l_done"], 1)
                    else:
                        dve.wait_ge(s["shift_done"], 2 * p + k - 1)
                    dve.scalar_tensor_tensor(out=t_lo[:, k], in0=halves[4 + k] if k < 2 else a_g[:, k - 2],
                                             scalar=2.0 ** -6, in1=t_hi[:, k],
                                             op0=ALU.mult, op1=ALU.subtract).then_inc(s["t_lo_done"], 1)

                def neg_g_tile(j):
                    dve.wait_ge(s["t_mm"], 4 * p + 3 + j)
                    for c in range(OC):
                        last = dve.scalar_tensor_tensor(out=diag_junk[:, 4 + 2 * j + c, :],
                                                        in0=halves[6 + j][:, c, c * P:(c + 1) * P], scalar=-1.0,
                                                        in1=ident[:], op0=ALU.mult, op1=ALU.mult,
                                                        accum_out=neg_g[:, 2 * j + c:2 * j + c + 1])
                    last.then_inc(s["neg_g_done"], 1)

                def t_rows():
                    for j, b in ((0, 7), (1, 4)):
                        dve.wait_ge(s["k_mm"], 2 * q + j + 1)
                        dve.tensor_scalar(a_row[:, j, :], bank[b][:], q_max[:, j:j + 1], 0.0, ALU.add, ALU.min)
                        dve.tensor_scalar(b_row[:, j, :], bank[b][:], q_max[:, j:j + 1], 0.0, ALU.add, ALU.max)\
                           .then_inc(s["t_done"], 1)

                def att_tile(g):
                    j, n = g // NC, g % NC
                    dve.wait_ge(s["vb_done"], 8 * q + g + 1)
                    wait(dve, s["att_lo_done"], 8 * q + g - 1)
                    dve.scalar_tensor_tensor(out=att[:, g % 2, :], in0=a_row[:, j, :], scalar=u_col[:, j, n:n + 1],
                                             in1=vb[:, g % 2, :], op0=ALU.mult, op1=ALU.max)\
                       .then_inc(s["att_done"], 1)

                for g in range(8 + 5):
                    if l1 and g < 8:
                        dve.wait_ge(s["z_hi_done"], 8 * p + g + 1)
                        dve.tensor_tensor(z_lo[:, g, :], bank[g % 4][:], z_hi[:, g, :], ALU.subtract)\
                           .then_inc(s["z_lo_done"], 1)
                    if l1 and not at(p, 0):
                        if g < 2:
                            o_stat_tile(p - 1, 2 * g)
                            o_stat_tile(p - 1, 2 * g + 1)
                        if g == 1:
                            o_mean(p - 1)
                        if g == 4:
                            o_norm(p - 1)
                    if l0 and g == 3:
                        t_rows()
                    if l0 and g >= 5:
                        att_tile(g - 5)
                    if l1 and g in T_LO_AT:
                        t_lo_tile(T_LO_AT.index(g))
                    if l1 and g == 11:
                        dve.wait_ge(s["sq_l_done"], 2 * p + 2)
                        dve.tensor_scalar(sq_lc[:], sq_l[:], c_norm[:, 0:1], None, ALU.max)\
                           .then_inc(s["sq_lc_done"], 1)
                        neg_g_tile(0)
                    if at(p, -1):
                        if g == 3:
                            gram_top(0)
                            gram_scales(0)
                        if g == 6:
                            u_lo(0)
                        if g == 9:
                            gram_top(1)
                        if g == 10:
                            gram_scales(1)
                        if g == 12:
                            wvo_top((0, 1, 2))
                            u_lo(1)

                def split_x():
                    dve.wait_ge(s["x_loaded"], 16 * (r + 1))
                    wait(dve, s["wx_mm"], 8 * r)
                    for j in range(2):
                        dve.tensor_copy(x_hi[:, j], x_in[:, j]).then_inc(s["x_hi_done"], 1)
                        if at(p, -2):
                            dve.wait_ge(s["x_hi_done"], j + 1)
                            dve.tensor_tensor(x_lo[:, j], x_in[:, j], x_hi[:, j], ALU.subtract)\
                               .then_inc(s["x_lo_done"], 1)

                if at(p, -2):
                    split_x()
                if l1:
                    neg_g_tile(1)
                    for k in range(len(T_LO_AT), 4):
                        t_lo_tile(k)
                    v_lo_tile(0)
                    dve.wait_ge(s["r_l_done"], p + 1)
                    for k in range(4):
                        last = dve.tensor_scalar(diag_r[:, k, :], ident[:], r_l[:, k:k + 1], None, ALU.mult)
                    last.then_inc(s["diag_r_done"], 1)
                    if l0:
                        v_lo_tile(1)
                    for j in range(2):
                        dve.wait_ge(s["s_mm"], 4 * p + 3 + j)
                        dve.wait_ge(s["neg_g_done"], 2 * p + j + 1)
                        for c in range(OC):
                            last = dve.tensor_scalar(a_g[:, j, c, :], halves[6 + j][:, c, :],
                                                     neg_g[:, 2 * j + c:2 * j + c + 1], 0.0, ALU.add, ALU.min)
                        last.then_inc(s["clamp_done"], 1)
                    if l0:
                        v_lo_tile(2)
                    for j in range(2):
                        dve.wait_ge(s["r_mm"], p + 1)
                        for c in range(OC):
                            last = dve.tensor_tensor(a_l[:, j, c, :], halves[3][:, j, :], mask[:, c, :], ALU.mult)
                        last.then_inc(s["mr_done"], 1)
                    if l0:
                        den(0)
                    for k in range(4):
                        j, c = k // 2, k % 2
                        dve.wait_ge(s["s_mm"], 4 * p + j + 1)
                        dve.wait_ge(s["mr_done"], 2 * p + j + 1)
                        last = dve.scalar_tensor_tensor(out=a_l[:, j, c, :], in0=halves[4 + j][:, c, :], scalar=0.0,
                                                        in1=a_l[:, j, c, :], op0=ALU.max, op1=ALU.mult,
                                                        accum_out=deg_l[:, k:k + 1])
                        if k == 1 and l0:
                            den(1)
                    last.then_inc(s["al_done"], 1)
                    if l0:
                        den(2)
                    for k in range(4):
                        j, c = k // 2, k % 2
                        dve.wait_ge(s["exp_done"], 2 * p + j + 1)
                        last = dve.scalar_tensor_tensor(out=a_g[:, j, c, :], in0=a_g[:, j, c, :], scalar=1.0,
                                                        in1=mask[:, c, :], op0=ALU.mult, op1=ALU.mult,
                                                        accum_out=deg_g[:, k:k + 1])
                    last.then_inc(s["ag_done"], 1)
                    if l0:
                        den(3)
                    dve.wait_ge(s["al_done"], p + 1)
                    dve.tensor_tensor(deg_l2[:], deg_l[:], r_l[:], ALU.mult).then_inc(s["dl_done"], 1)
                    dve.wait_ge(s["ag_done"], p + 1)
                    dve.tensor_scalar(deg_g2[:], deg_g[:], DEG_EPS, None, ALU.max).then_inc(s["dgr_done"], 1)
                    dve.wait_ge(s["dl_done"], 3 * p + 1)
                    dve.tensor_scalar(deg_l3[:], deg_l2[:], DEG_EPS, None, ALU.max).then_inc(s["dl_done"], 1)
                    dve.wait_ge(s["dgr_done"], 2 * p + 1)
                    dve.reciprocal(deg_g3[:], deg_g2[:]).then_inc(s["dgr_done"], 1)
                    dve.wait_ge(s["dl_done"], 3 * p + 2)
                    dve.reciprocal(deg_l4[:], deg_l3[:]).then_inc(s["dl_done"], 1)
                    dve.wait_ge(s["dgr_done"], 2 * p + 2)
                    dve.tensor_scalar(s_g[:], deg_g3[:], c_wg[:, 0:1], None, ALU.mult).then_inc(s["sg_done"], 1)
                    dve.wait_ge(s["dl_done"], 3 * p + 3)
                    dve.scalar_tensor_tensor(out=s_l[:], in0=deg_l4[:], scalar=c_wl[:, 0:1], in1=r_l[:],
                                             op0=ALU.mult, op1=ALU.mult).then_inc(s["sl_done"], 1)
                    if l0:
                        den(4)
                    dve.wait_ge(s["sl_done"], p + 1)
                    for k in range(4):
                        j, c = k // 2, k % 2
                        dve.tensor_scalar(a_l[:, j, c, :], a_l[:, j, c, :], s_l[:, k:k + 1], None, ALU.mult)\
                           .then_inc(s["kl_done"], 1)
                    dve.wait_ge(s["sg_done"], p + 1)
                    for k in range(4):
                        j, c = k // 2, k % 2
                        dve.wait_ge(s["kl_done"], 4 * p + k + 1)
                        last = dve.scalar_tensor_tensor(out=a_l[:, j, c, :], in0=a_g[:, j, c, :],
                                                        scalar=s_g[:, k:k + 1], in1=a_l[:, j, c, :],
                                                        op0=ALU.mult, op1=ALU.add)
                        if c == 1:
                            last.then_inc(s["k_done"], 1)
                            if l0:
                                den(5 + j)
                    if l0:
                        den(7)
                    else:
                        v_lo_tile(1)
                        v_lo_tile(2)
                        v_lo_tile(3)
                    for j in range(2):
                        dve.wait_ge(s["kt_hi_done"], 2 * p + j + 1)
                        dve.tensor_tensor(kt_lo[:, j], halves[4 + j], kt_hi[:, j], ALU.subtract)\
                           .then_inc(s["kt_lo_done"], 1)
                elif l0:
                    wvo_top((3,))
                    den(0)
                    scales((4, 5), s["topv_all"], s["scalev"], 4)
                    split_x()
                    den(1)
                    den(2)
                    wvo_lo_tiles()
                    for k in range(3, 8):
                        den(k)
                    constants()
                if l0:
                    def y_stat_tile(k):
                        if k % 2:
                            dve.wait_ge(s["y_odd_done"], 2 * q + k // 2 + 1)
                        else:
                            dve.wait_ge(s["y_done"], 2 * q + k // 2 + 1)
                        dve.bn_stats(y_stat[:, k, :], y[:, k, :]).then_inc(s["y_stat_done"], 1)

                    if x_first:
                        dve.wait_ge(s["uv_done"], r)
                    dve.wait_ge(s["xr_loaded"], 16 * (q + 1))
                    for k in (0, 2):
                        dve.wait_ge(s["relu_done"], 4 * q + k + 1)
                        dve.tensor_tensor(y[:, k, :], y[:, k, :], x_res[:, k // 2, k % 2, :], ALU.add)\
                           .then_inc(s["y_done"], 1)
                        y_stat_tile(k)
                    y_stat_tile(1)
                    if x_first:
                        xw_lo_tile(0)
                        xw_lo_tile(1)
                    if l1:
                        v_lo_tile(3)
                    y_stat_tile(3)
                    wait(dve, s["y_rstd_done"], q)
                    dve.wait_ge(s["y_stat_done"], 4 * q + 4)
                    dve.tensor_scalar(turn_y[:], y_stat[:, 3, 0:1], 1.0, None, ALU.mult)
                    for k in range(4):
                        last = dve.bn_aggr(y_mv[:, k, :], y_stat[:, k, :])
                    last.then_inc(s["y_mv_done"], 1)
                    if x_first:
                        xw_lo_tile(2)
                        xw_lo_tile(3)

                def residual(k):
                    dve.wait_ge(s["o_mm"], 4 * p + k + 1)
                    dve.scalar_tensor_tensor(out=o[:, k, :], in0=bank[late[k]][:], scalar=c_out[:, 0:1],
                                             in1=h[:, k, :], op0=ALU.mult, op1=ALU.add).then_inc(s["o_done"], 1)

                def h_tile(k):
                    if k == 0:
                        dve.wait_ge(s["y_rstd_done"], q + 1)
                        dve.wait_ge(s["y_mv_done"], q + 1)
                    wait(dve, s["o_done"], 4 * p + k + 1)
                    dve.tensor_scalar(h[:, k, :], y[:, k, :], y_mv[:, k, 0:1], y_rstd[:, k:k + 1],
                                      ALU.subtract, ALU.mult).then_inc(s["h_done"], 1)

                if l1:
                    wait(dve, s["stored"], 32 * p)
                for k in range(4 + 1):
                    if l1 and k < 4:
                        residual(k)
                        if not l0:
                            o_stat_tile(p, k)
                    if l0 and k >= 1:
                        h_tile(k - 1)
                if new:
                    wait(dve, s["uv_done"], r)
                    for k in range(4, 8) if x_first else range(4):
                        xw_lo_tile(k)
                if l0:
                    for d in range(DC):
                        dve.wait_ge(s["ht_hi_done"], 4 * q + d + 1)
                        dve.tensor_tensor(ht_lo[:, d, :], bank[d][:], ht_hi[:, d, :], ALU.subtract)\
                           .then_inc(s["ht_lo_done"], 1)
                if new and not x_first:
                    for k in range(4, 8):
                        xw_lo_tile(k)
                if new:
                    dve.wait_ge(s["xw_lo_done"], 8 * r + 8)
                    dve.tensor_reduce(q_part[:], q_cols, AX.X, ALU.max).then_inc(s["q_part_done"], 1)
                    dve.tensor_copy(k_hi[:], qk[:, :, 1]).then_inc(s["k_hi_done"], 1)
                    dve.wait_ge(s["k_hi_done"], r + 1)
                    dve.tensor_tensor(k_lo[:], qk[:, :, 1], k_hi[:], ALU.subtract).then_inc(s["k_lo_done"], 1)
                    for n in range(2 * NC):
                        last = dve.tensor_scalar(dk_hi[:, n, :], ident16[:], k_hi[:, n:n + 1], None, ALU.mult)
                    last.then_inc(s["dk_hi_done"], 1)
                    dve.wait_ge(s["q_max_done"], r + 1)
                    wait(dve, s["uv_done"], r)
                    for j in range(2):
                        last = dve.tensor_scalar(q_rel[:, j, :], q_cols[:, j, :], q_max[:, j:j + 1], None, ALU.subtract)
                    last.then_inc(s["q_rel_done"], 1)

            setup0()
            pipeline(dve, step)
            o_mean(PAIRS - 1)
            o_norm(PAIRS - 1)

        @block.gpsimd
        def _(pool):
            pool.memset(ident[:], 0.0).then_inc(s["pool_set"], 1)
            pool.memset(exponent[:], -0.5).then_inc(s["pool_set"], 1)
            pool.memset(top_part[:, 5:8], 0.0).then_inc(s["pool_set"], 1)
            pool.memset(eps[:], LN_EPS).then_inc(s["pool_set"], 1)
            pool.wait_ge(s["pool_set"], 4)
            pool.affine_select(out=ident[:], in_=ident[:], compare_op=ALU.not_equal, fill=1.0, base=0,
                               pattern=[[-1, P]], channel_multiplier=1).then_inc(s["pool_set"], 1)

            def largest(cols, ready, done):
                pool.wait_ge(ready, 1)
                pool.partition_all_reduce(top_all[:, cols[0]:cols[1]], top_part[:, cols[0]:cols[1]], P, RMAX)\
                    .then_inc(done, 1)

            def cut_mask():
                pool.wait_ge(s["mask_loaded"], 16)
                pool.affine_select(out=mask[:], in_=mask[:], compare_op=ALU.not_equal, fill=0.0, base=0,
                                   pattern=[[P, OC], [-1, O]], channel_multiplier=1).then_inc(s["mask_cut"], 1)

            def step(p, l1, l0, new):
                q, r = p + 1, p + 2
                if l0:
                    wait(pool, s["ot_mm"], 8 * q)
                    for g in range(8):
                        pool.wait_ge(s["att_hi_done"], 8 * q + g + 1)
                        n = (g // NC, g % NC)
                        pool.tensor_tensor(att_lo[:, n[0], n[1], :], att[:, g % 2, :], att_hi[:, n[0], n[1], :],
                                           ALU.subtract).then_inc(s["att_lo_done"], 1)
                        if at(p, -1) and g == 3:
                            largest((3, 4), s["top_g"], s["top_g_all"])
                if l1:
                    pool.wait_ge(s["sq_lc_done"], p + 1)
                    wait(pool, s["sl_done"], p)
                    pool.tensor_tensor(r_l[:], sq_lc[:], exponent[:], ALU.pow).then_inc(s["r_l_done"], 1)
                if new:
                    if at(p, -1):
                        largest((4, 5), s["topv"], s["topv_all"])
                    wait(pool, s["wx_mm"], 8 * r)
                    for j in range(0 if at(p, -2) else 2):
                        pool.wait_ge(s["x_hi_done"], 2 * r + j + 1)
                        pool.tensor_tensor(x_lo[:, j], x_in[:, j], x_hi[:, j], ALU.subtract)\
                            .then_inc(s["x_lo_done"], 1)
                if l0:
                    pool.wait_ge(s["xr_loaded"], 16 * (q + 1))
                    for k in (1, 3):
                        pool.wait_ge(s["relu_done"], 4 * q + k + 1)
                        pool.tensor_tensor(y[:, k, :], y[:, k, :], x_res[:, k // 2, k % 2, :], ALU.add)\
                            .then_inc(s["y_odd_done"], 1)
                    pool.wait_ge(s["y_mv_done"], q + 1)
                    pool.tensor_tensor(y_var[:], y_mv[:, :, 1], eps[:], ALU.add).then_inc(s["y_var_done"], 1)
                    pool.wait_ge(s["y_var_done"], q + 1)
                    wait(pool, s["h_done"], 4 * q)
                    pool.tensor_tensor(y_rstd[:], y_var[:], exponent[:], ALU.pow).then_inc(s["y_rstd_done"], 1)
                if new:
                    pool.wait_ge(s["q_part_done"], r + 1)
                    pool.tensor_tensor(turn_q[:], q_part[:], q_part[:], ALU.add)
                    pool.partition_all_reduce(q_max[:], q_part[:], P, RMAX).then_inc(s["q_max_done"], 1)
                if at(p, -2):
                    largest((2, 3), s["top_l"], s["top_l_all"])
                    cut_mask()
                if l1:
                    pool.wait_ge(s["o_mv_done"], p + 1)
                    pool.tensor_tensor(o_var[:], o_mv[:, :, 1], eps[:], ALU.add).then_inc(s["o_var_done"], 1)
                    pool.wait_ge(s["o_var_done"], p + 1)
                    wait(pool, s["normed"], 2 * p)
                    pool.tensor_tensor(o_rstd[:], o_var[:], exponent[:], ALU.pow).then_inc(s["o_rstd_done"], 1)

            largest((0, 2), s["top0"], s["top0_all"])
            pipeline(pool, step)


_SHAPE = (32, 256, 512)


def kernel(**inputs):
    import numpy as np
    import concourse.bacc as bacc
    from concourse.bass_utils import run_bass_kernel_spmd

    a = {k: np.asarray(v) for k, v in inputs.items()}
    laid = {
        "x": a["x"],
        "adj": a["adj"],
        "adjT": a["adj"].T,
        "wqk": np.stack([a["L0_gnn_wq"], a["L0_gnn_wk"]], -1).reshape(2, P, 2).transpose(1, 0, 2),
        "bm": a["L0_gnn_bm"].reshape(2, P).T,
        "wl": a["L1_gnn_W_lang"],
        "wg": a["L1_gnn_W_grav"],
        "wv": a["L1_gnn_W_V"],
        "woT": a["L1_gnn_W_O"].T,
        "gate": np.broadcast_to(a["L1_gnn_gate_logit"].reshape(1, 1), (P, 1)),
        "sigma": np.broadcast_to(a["L1_gnn_log_sigma"].reshape(1, 1), (P, 1)),
    }
    nc = bacc.Bacc("TRN2", target_bir_lowering=False, num_devices=1)
    arrays, args = {}, []
    for name, v in laid.items():
        v = np.ascontiguousarray(v)
        arrays[f"in_{name}"] = v
        args.append(nc.dram_tensor(f"in_{name}", v.shape, mybir.dt.from_np(v.dtype), kind="ExternalInput").ap())
    args.append(nc.dram_tensor("out_y", _SHAPE, F32, kind="ExternalOutput").ap())
    build(nc, *args)
    r = run_bass_kernel_spmd(nc, [arrays], core_ids=[0])
    return r.results[0]["out_y"]
```
